# Optimizing a Trainium2 kernel written in Bass

```python
import numpy as np
import jax
import jax.numpy as jnp

def _softmax(x, axis=-1):
    return jax.nn.softmax(x, axis=axis)

def _gelu(x):
    return jax.nn.gelu(x, approximate=True)

def _silu(x):
    return jax.nn.silu(x)

def _sigmoid(x):
    return jax.nn.sigmoid(x)

def _layernorm(x, axis=-1, eps=1e-05):
    m = jnp.mean(x, axis=axis, keepdims=True)
    v = jnp.var(x, axis=axis, keepdims=True)
    return (x - m) / jnp.sqrt(v + eps)

def _scatter_add(tgt, idx, src, axis=0):
    return tgt.at[idx].add(src)

def _segment_sum(src, seg, n):
    return jax.ops.segment_sum(src, seg, n)
kernel_name = 'mk_flamingo_gated_d1_seqx_r8_f524fb'

def setup_inputs(seed: int=0):
    np.random.seed(seed)
    _w = jnp.asarray

    def _rec_inputs():
        import jax
        import jax.numpy as jnp
        _rk = jax.random.key(seed)
        x = 2.818e-05 + 1 * jax.random.normal(jax.random.fold_in(_rk, 1), (4, 256, 256), jnp.float32)
        _lenS = 256 - jax.random.randint(jax.random.fold_in(_rk, 7), (4,), 0, max(1, 256 // 4) + 1, jnp.int32)
        _lenS2 = 256 - jax.random.randint(jax.random.fold_in(_rk, 8), (4,), 0, max(1, 256 // 4) + 1, jnp.int32)
        _ctx_1024P = jax.random.normal(jax.random.fold_in(_rk, 11), (4, 16, 128), jnp.float32)
        _ctx_1024c = jax.random.dirichlet(jax.random.fold_in(_rk, 511), 0.3 * jnp.ones((16,), jnp.float32), (4, 256))
        _ctx_1024t = jnp.einsum('bsk,bkd->bsd', _ctx_1024c, _ctx_1024P)
        _ctx_1024t = _ctx_1024t * jax.lax.rsqrt(jnp.mean(jnp.square(_ctx_1024t)) + 1e-12) * 0.953939
        ctx_1024 = 7.22013e-05 + 1.00017 * (_ctx_1024t + 0.3 * jax.random.normal(jax.random.fold_in(_rk, 611), (4, 256, 128), jnp.float32))
        _g = jax.random.normal(jax.random.fold_in(_rk, 9001), (2, 1), jnp.float32)
        _g = jnp.sign(_g) * jnp.maximum(jnp.abs(_g), 1.0) + (_g == 0) * 1.0
        g_xattn = _g[0]
        g_ffn = _g[1]
        return (x, ctx_1024, g_xattn, g_ffn)
    x, ctx_1024, g_xattn, g_ffn = _rec_inputs()

    def _L0_xattn_setup():
        import jax, jax.numpy as jnp
        import numpy as np
        B_, L_, D_MODEL = (4, 256, 128)
        D_STATE, D_CONV, EXPAND = (16, 4, 2)
        D_INNER = EXPAND * D_MODEL
        DT_RANK = (D_MODEL + 15) // 16

        def silu(x):
            return x * jax.nn.sigmoid(x)
        key = jax.random.key(seed)
        ks = jax.random.split(key, 10)
        f32 = jnp.float32
        hidden_states = jax.random.normal(ks[0], (B_, L_, D_MODEL), dtype=f32)
        z = jax.random.normal(ks[1], (B_, D_INNER, L_), dtype=f32)
        in_proj_w = jax.random.normal(ks[2], (D_INNER, D_MODEL), dtype=f32) * 0.02
        conv_w = jax.random.normal(ks[3], (D_INNER, 1, D_CONV), dtype=f32) * 0.1
        conv_b = jax.random.normal(ks[4], (D_INNER,), dtype=f32) * 0.02
        x_proj_w = jax.random.normal(ks[5], (DT_RANK + 2 * D_STATE, D_INNER), dtype=f32) * 0.02
        dt_proj_w = jax.random.uniform(ks[6], (D_INNER, DT_RANK), dtype=f32, minval=-DT_RANK ** (-0.5), maxval=DT_RANK ** (-0.5))
        dt = jnp.exp(jax.random.uniform(ks[7], (D_INNER,), dtype=f32, minval=np.log(0.001), maxval=np.log(0.1)))
        dt_proj_b = jnp.log(jnp.expm1(dt))
        A_log = jnp.log(jnp.broadcast_to(jnp.arange(1, D_STATE + 1, dtype=f32), (D_INNER, D_STATE)))
        D = jnp.ones((D_INNER,), f32)
        return {'hidden_states': hidden_states, 'z': z, 'in_proj_w': in_proj_w, 'conv_w': conv_w, 'conv_b': conv_b, 'x_proj_w': x_proj_w, 'dt_proj_w': dt_proj_w, 'dt_proj_b': dt_proj_b, 'A_log': A_log, 'D': D}
    _L0_xattn_all = _L0_xattn_setup()
    _L0_xattn_in = {k: v for k, v in _L0_xattn_all.items() if k in ('in_proj_w', 'conv_w', 'conv_b', 'x_proj_w', 'dt_proj_w', 'dt_proj_b', 'A_log', 'D')}
    del _L0_xattn_all

    def _L0_ffn_setup():
        import jax, jax.numpy as jnp
        import numpy as np
        NORM_EPS = 1e-05

        def _quant_input(x):
            s = 127.0 / jnp.clip(jnp.max(jnp.abs(x), axis=-1, keepdims=True), 1e-05, None)
            return jnp.clip(jnp.round(x * s), -128.0, 127.0) / s

        def _rmsnorm(x, w, eps):
            return x * jax.lax.rsqrt(jnp.mean(x * x, axis=-1, keepdims=True) + eps) * w
        key = jax.random.key(seed)
        k0, k1, k2 = jax.random.split(key, 3)
        dim, hidden = (256, 704)
        x = jax.random.normal(k0, (4, 256, dim), dtype=jnp.float32)
        w13 = jax.random.normal(k1, (2 * hidden, dim), dtype=jnp.float32) * 0.02
        w2 = jax.random.normal(k2, (dim, hidden), dtype=jnp.float32) * 0.02
        norm_w = jnp.ones((hidden,), dtype=jnp.float32)
        return {'x': x, 'w13': w13, 'w2': w2, 'norm_w': norm_w}
    _L0_ffn_all = _L0_ffn_setup()
    _L0_ffn_in = {k: v for k, v in _L0_ffn_all.items() if k in ('w13', 'w2', 'norm_w')}
    del _L0_ffn_all
    return {'x': x, 'ctx_1024': ctx_1024, 'g_xattn': g_xattn, 'g_ffn': g_ffn, 'L0_xattn_in_proj_w': _L0_xattn_in['in_proj_w'], 'L0_xattn_conv_w': _L0_xattn_in['conv_w'], 'L0_xattn_conv_b': _L0_xattn_in['conv_b'], 'L0_xattn_x_proj_w': _L0_xattn_in['x_proj_w'], 'L0_xattn_dt_proj_w': _L0_xattn_in['dt_proj_w'], 'L0_xattn_dt_proj_b': _L0_xattn_in['dt_proj_b'], 'L0_xattn_A_log': _L0_xattn_in['A_log'], 'L0_xattn_D': _L0_xattn_in['D'], 'L0_ffn_w13': _L0_ffn_in['w13'], 'L0_ffn_w2': _L0_ffn_in['w2'], 'L0_ffn_norm_w': _L0_ffn_in['norm_w']}

def reference(x, ctx_1024, g_xattn, g_ffn, L0_xattn_in_proj_w, L0_xattn_conv_w, L0_xattn_conv_b, L0_xattn_x_proj_w, L0_xattn_dt_proj_w, L0_xattn_dt_proj_b, L0_xattn_A_log, L0_xattn_D, L0_ffn_w13, L0_ffn_w2, L0_ffn_norm_w):
    import jax
    import jax.numpy as jnp

    def _L0_xattn_ref(hidden_states, z, in_proj_w, conv_w, conv_b, x_proj_w, dt_proj_w, dt_proj_b, A_log, D):
        import jax, jax.numpy as jnp
        import numpy as np
        B_, L_, D_MODEL = (4, 256, 128)
        D_STATE, D_CONV, EXPAND = (16, 4, 2)
        D_INNER = EXPAND * D_MODEL
        DT_RANK = (D_MODEL + 15) // 16

        def silu(x):
            return x * jax.nn.sigmoid(x)
        Bsz, L, _ = hidden_states.shape
        d_inner, _, d_conv = conv_w.shape
        dt_rank = dt_proj_w.shape[1]
        d_state = A_log.shape[1]
        x = jnp.einsum('bld,ed->bel', hidden_states, in_proj_w)
        xc = jax.lax.conv_general_dilated(x, conv_w, window_strides=(1,), padding=[(d_conv - 1, 0)], feature_group_count=d_inner, dimension_numbers=('NCH', 'OIH', 'NCH'))
        x = silu(xc + conv_b[None, :, None])
        x_dbl = jnp.einsum('bdl,ed->bel', x, x_proj_w)
        dt_low, Bm, Cm = jnp.split(x_dbl, [dt_rank, dt_rank + d_state], axis=1)
        dt = jnp.einsum('brl,dr->bdl', dt_low, dt_proj_w)
        dt = jax.nn.softplus(dt + dt_proj_b[None, :, None])
        A = -jnp.exp(A_log)
        dt_t = jnp.moveaxis(dt, -1, 0)
        B_t = jnp.moveaxis(Bm, -1, 0)
        C_t = jnp.moveaxis(Cm, -1, 0)
        u_t = jnp.moveaxis(x, -1, 0)

        def step(state, inp):
            d, b, c, u = inp
            dA = jnp.exp(d[..., None] * A)
            state = state * dA + (d * u)[..., None] * b[:, None, :]
            y = jnp.einsum('bdn,bn->bd', state, c)
            return (state, y)
        state0 = jnp.zeros((Bsz, d_inner, d_state), x.dtype)
        _, ys = jax.lax.scan(step, state0, (dt_t, B_t, C_t, u_t))
        y = jnp.moveaxis(ys, 0, 2)
        y = y + D[None, :, None] * x
        y = y * silu(z)
        return jnp.swapaxes(y, 1, 2)

    def _L0_ffn_ref(x, w13, w2, norm_w):
        import jax, jax.numpy as jnp
        import numpy as np
        NORM_EPS = 1e-05

        def _quant_input(x):
            s = 127.0 / jnp.clip(jnp.max(jnp.abs(x), axis=-1, keepdims=True), 1e-05, None)
            return jnp.clip(jnp.round(x * s), -128.0, 127.0) / s

        def _rmsnorm(x, w, eps):
            return x * jax.lax.rsqrt(jnp.mean(x * x, axis=-1, keepdims=True) + eps) * w
        xq = _quant_input(x)
        x13 = jnp.einsum('bsd,fd->bsf', xq, w13)
        x1, x3 = jnp.split(x13, 2, axis=-1)
        gated = jnp.square(jax.nn.relu(x1)) * x3
        inner = _rmsnorm(gated, norm_w, NORM_EPS)
        iq = _quant_input(inner)
        out = jnp.einsum('bsh,dh->bsd', iq, w2)
        return out
    x = x + jnp.tanh(g_xattn[0]) * _L0_xattn_ref(ctx_1024, _layernorm(x, axis=-1), L0_xattn_in_proj_w, L0_xattn_conv_w, L0_xattn_conv_b, L0_xattn_x_proj_w, L0_xattn_dt_proj_w, L0_xattn_dt_proj_b, L0_xattn_A_log, L0_xattn_D)
    x = x + jnp.tanh(g_ffn[0]) * _L0_ffn_ref(_layernorm(x, axis=-1), L0_ffn_w13, L0_ffn_w2, L0_ffn_norm_w)
    return x

_drawn_inputs = setup_inputs


def setup_inputs(seed=0):
    import zlib

    import numpy as np

    out = dict(_drawn_inputs(seed))
    spreads = {'L0_xattn_D': (1.0, 0.6), 'L0_ffn_norm_w': (1.0, 0.6)}
    factors = {'ctx_1024': 3.839,
     'L0_xattn_in_proj_w': 3.589,
     'L0_xattn_conv_w': 3.796,
     'L0_xattn_conv_b': 5.733,
     'L0_xattn_x_proj_w': 8.0,
     'L0_xattn_dt_proj_w': 8.0,
     'L0_xattn_dt_proj_b': 8.0,
     'L0_xattn_A_log': 8.0,
     'L0_ffn_w13': 8.0,
     'L0_ffn_w2': 8.0}
    for name, (base, spread) in spreads.items():
        noise = np.random.default_rng([zlib.crc32(name.encode()), seed]).standard_normal(out[name].shape)
        drawn = base * np.exp(spread * noise) if base else spread * noise
        out[name] = jnp.asarray(drawn.astype(out[name].dtype))
    for name, factor in factors.items():
        out[name] = (out[name] * factor).astype(out[name].dtype)
    return out
```

```python
import concourse.bass as bass
from concourse import mybir
from contextlib import ExitStack

fp32 = mybir.dt.float32
bf16 = mybir.dt.bfloat16
ALU = mybir.AluOpType
ACT = mybir.ActivationFunctionType
AX = mybir.AxisListType

P = 128
BATCH, L, DI = 4, 256, 256
DM = 128
NS, RANK, TAPS = 16, 8, 4
HALVES = DI // P
GN = 4
NG = NS // GN
HID = 704
HPAD = 768
FB = HPAD // P
UC = HID // 2
EPS = 1e-5
MAGIC = 1.5 * 2.0 ** 23
SMALL = 2.0 ** -8
CLAMP = 2.0 ** 60
BANK = 512
NWORK = 3
NWP = 9

GT = 4
TICKS = GT * NG
CORE = [
    ("bc_b", "pe", -2), ("bc_c", "pe", -1), ("decay0", "act", -1), ("c_copy", "act", 0), ("mix0", "dve", 0),
    ("decay1", "act", 1), ("mix1", "dve", 1), ("scan0", "dve", 2), ("scan1", "dve", 3), ("out0", "pool", 3),
    ("out1", "pool", 4), ("sum0", "pe", 5), ("sum1", "pe", 6),
]
def chain(b):
    first, last = b == 0, b == BATCH - 1
    early, late = ("dve" if first else "pool"), ("dve" if last else "pool")
    steps = [
        ("ctxT", 0, "pe", -18), ("ctxT", 0, "act", -17), ("inproj", 0, "pe", -16), ("conv", 0, "dve", -15),
        ("sigm0", 0, "act", -14), ("clamp", 0, "dve", -13), ("sigm1", 0, "act", -12), ("u", 0, early, -11),
        ("xdbl", 0, "pe", -9), ("split", 0, "dve", -8), ("dtproj", 0, "pe", -8), ("absx", 0, "act", -7),
        ("series", 0, "dve", -5), ("ln1q", 0, "act", -4), ("dt", 0, "dve", -3), ("du", 0, early, -2),
        ("z", 0, "dve", 4 if first else -7), ("zsig", 0, "act", 5 if first else -6),
        ("sz", 0, "pool", 7 if first else -4),
        ("yd", 0, "dve", 19), ("yz", 0, late, 20), ("yT", 0, "pe", 22), ("x1", 0, "dve", 23),
        ("rs1", 0, "act", 24), ("quant1", 0, "dve", 25), ("xqT", 0, "pe", 26), ("xqT", 0, "act", 27),
    ]
    for i in range(2 * HALVES):
        steps += [("up", i, "pe", 28 + i), ("relu", i, "act", 29 + i), ("gate", i, "dve", 30 + i)]
        if i % 2:
            steps.append(("gated", i // 2, late, 31 + i))
    for i in range(HALVES):
        steps += [("square", i, "act", 34 + 2 * i), ("absmax", i, "dve", 34 + 2 * i)]
        if last:
            steps += [("rs2", i, "act", 35 + 2 * i), ("scale2", i, "dve", 36 + 2 * i), ("quant2", i, "dve", 36 + 2 * i)]
        else:
            steps += [("quant2", i, "dve", 38 + i)]
    if not last:
        steps += [("rs2", 0, "act", 37), ("scale2", 0, "dve", 37.5)]
    for i in range(HALVES):
        steps += [("iqT", i, "pe", 39 + i), ("iqT", i, "act", 40 + i), ("down", i, "pe", 41 + i), ("final", i, "dve", 42 + i)]
    return steps


ONCE = [("setup", 0, e, -100) for e in ("pe", "act", "dve")]
ONCE += [("sel", 0, "act", -16), ("xstat", 0, "dve", 1), ("xrs", 0, "act", 2), ("gates", 0, "dve", 3)]
for _i in range(NWP):
    ONCE += [("w", _i, "pe", _i - 12), ("w_hi", _i, "act", _i - 11), ("w_res", _i, "dve", _i - 10),
             ("w_mid", _i, "act", _i - 9), ("w_lo", _i, "pool", _i - 8)]
FILLS = {
    "setup": [("setup", "act"), ("setup", "act"), ("setup", "dve")], "w": [("w_res", "dve")],
    "ctxT": [("ctxT", "act")], "inproj": [("conv", "dve")], "xdbl": [("split", "dve")], "dtproj": [("absx", "act")],
    "yT": [("x1", "dve")], "xqT": [("xqT", "act")], "up": [("relu", "act"), ("gate", "dve")],
    "iqT": [("iqT", "act"), ("iqT", "act")], "down": [("final", "dve")],
}


def schedule():
    timed = [(t, name, e, 0, i) for name, i, e, t in ONCE]
    for b in range(BATCH):
        for name, i, e, t in chain(b):
            timed.append((TICKS * b + t, name, e, b, i))
        for g in range(NG):
            for name, e, t in CORE:
                timed.append((TICKS * b + GT * g + t, name, e, b, g))
    timed.sort(key=lambda s: s[0])
    return {e: [(name, b, i) for _, name, en, b, i in timed if en == e] for e in ("pe", "act", "dve", "pool")}


ORDER = schedule()


def number_banks():
    number = {}
    for name, b, i in ORDER["pe"]:
        for n in range(len(FILLS.get(name, []))):
            number[(name, b, i, n)] = len(number)
    by = [None] * len(number)
    for e in ("act", "dve"):
        count = 0
        for step, b, i in ORDER[e]:
            for name, fills in FILLS.items():
                for n, consumer in enumerate(fills):
                    if consumer == (step, e) and (name, b, i, n) in number:
                        count += 1
                        by[number[(name, b, i, n)]] = (e, count)
    return number, by


WORK_AT, WORK_BY = number_banks()


def build(nc, a, out):
    ctx = ExitStack()
    with ctx:
        def sb(name, shape, dt=fp32):
            return ctx.enter_context(nc.sbuf_tensor(name, shape, dt))

        def sem(name):
            return ctx.enter_context(nc.semaphore(name))

        identf = sb("identf", [P, P])
        pick = sb("pick", [P, 2 * NS])
        sel = sb("sel", [P, 2 * NS, P], bf16)
        ctx_in = sb("ctx_in", [P, BATCH * HALVES, DM])
        ctxT = sb("ctxT", [P, 2, L])
        win_in = sb("win_in", [P, HALVES, DM])
        winT = sb("winT", [P, DI])
        xpw_in = sb("xpw_in", [P, DI])
        xpwT = sb("xpwT", [P, HALVES, P])
        dtw_in = sb("dtw_in", [P, HALVES, RANK])
        dtwT = sb("dtwT", [RANK, DI])
        convw = sb("convw", [P, HALVES, TAPS])
        convb = sb("convb", [P, HALVES])
        dtb = sb("dtb", [P, HALVES])
        dskip = sb("dskip", [P, HALVES])
        nega = sb("nega", [P, HALVES, NS])
        gates = sb("gates", [P, 2])
        gtmp = sb("gtmp", [P, 2])
        normw = sb("normw", [P, HID])
        x = sb("x", [P, BATCH, HALVES, L])
        xstat = sb("xstat", [P, BATCH * HALVES, 6])
        xmv = sb("xmv", [P, BATCH * HALVES, 2])
        xrs = sb("xrs", [P, BATCH * HALVES])
        xt1 = sb("xt1", [P, BATCH * HALVES])
        xc = sb("xc", [P, 2, HALVES, L])
        sg = sb("sg", [P, 2, HALVES, L])
        u = sb("u", [P, 2, HALVES, L])
        bcs = sb("bcs", [P, 2, L], bf16)
        bcr = sb("bcr", [P, 2, L])
        dtlow = sb("dtlow", [RANK, 2, L])
        xs = sb("xs", [P, 2, HALVES, L])
        q = sb("q", [P, 2, HALVES, L])
        lw = sb("lw", [P, 2, HALVES, L])
        rr = sb("rr", [P, 2, HALVES, L])
        dt = sb("dt", [P, 2, HALVES, L])
        du = sb("du", [P, 2, HALVES, L])
        lnsmall = sb("lnsmall", [P, 1])
        zn = sb("zn", [P, 2, HALVES, L])
        ze = sb("ze", [P, 2, HALVES, L])
        yd = sb("yd", [P, 2, HALVES, L])
        dA = sb("dA", [P, 2, HALVES, GN, L])
        hb = sb("hb", [P, 3, HALVES, GN * L])
        cs = sb("cs", [P, 2, GN * L])
        fstat = sb("fstat", [P, HALVES, 6])
        fmv = sb("fmv", [P, HALVES, 2])
        frs = sb("frs", [P, HALVES])
        fam = sb("fam", [P, HALVES])
        finv = sb("finv", [P, HALVES])
        fs = sb("fs", [P, HALVES])
        xn = sb("xn", [P, HALVES, L])
        xqT = sb("xqT", [P, HALVES, HALVES, P], bf16)
        ru = sb("ru", [P, HALVES, HPAD])
        gg = sb("gg", [P, HALVES, HID])
        gw = sb("gw", [P, HALVES, HID])
        ssq = sb("ssq", [P, HALVES])
        gv = sb("gv", [P, HALVES])
        grs = sb("grs", [P, HALVES])
        gt = sb("gt", [P, HALVES])
        gam = sb("gam", [P, HALVES])
        gc = sb("gc", [P, HALVES])
        gos = sb("gos", [P, BATCH, HALVES])
        iqT = sb("iqT", [P, HALVES, FB, P], bf16)
        fin = sb("fin", [P, 2, L])
        w13_in = sb("w13_in", [P, 11, DI])
        w2_in = sb("w2_in", [P, HALVES, HPAD])
        w13T = sb("w13T", [P, 3, HALVES, 2 * HID], bf16)
        w2T = sb("w2T", [P, 3, FB * DI], bf16)
        wres = sb("wres", [P, 3, BANK])

        b_ps = ctx.enter_context(nc.psum_tensor("b_ps", [P, 2, BANK], fp32))
        c_ps = ctx.enter_context(nc.psum_tensor("c_ps", [P, 2, BANK], fp32))
        y_ps = ctx.enter_context(nc.psum_tensor("y_ps", [P, HALVES, L], fp32))
        w_ps = ctx.enter_context(nc.psum_tensor("w_ps", [P, NWORK, BANK], fp32))

        l_ctx0, l_ctx, l_win, l_small, l_x, l_w13, l_w2, l_nw, l_g = (
            sem(n) for n in ("l_ctx0", "l_ctx", "l_win", "l_small", "l_x", "l_w13", "l_w2", "l_nw", "l_g"))
        pool_k = sem("pool_k")
        act_k = sem("act_k")
        dve_k = sem("dve_k")
        pool_c = sem("pool_c")
        sel_ok = sem("sel_ok")
        work_full = sem("work_full")
        free = {"act": sem("work_free_act"), "dve": sem("work_free_dve")}
        winT_ok, dtwT_ok, nega_ok, gexp_ok = (sem(n) for n in ("winT_ok", "dtwT_ok", "nega_ok", "gexp_ok"))
        gates_ok, xmv_ok, xrs_ok = (sem(n) for n in ("gates_ok", "xmv_ok", "xrs_ok"))
        ctxT_ok, conv_e, clamp_ok, sig_ok, u_ok = (
            sem(n) for n in ("ctxT_ok", "conv_e", "clamp_ok", "sig_ok", "u_ok"))
        dtlow_ok, bcs_ok, abs_ok, q_ok, ql_ok, lw_ok, lns_ok, dt_ok, du_ok = (
            sem(n) for n in ("dtlow_ok", "bcs_ok", "abs_ok", "q_ok", "ql_ok", "lw_ok", "lns_ok", "dt_ok", "du_ok"))
        zn_ok, ze_ok, sz_ok = (sem(n) for n in ("zn_ok", "ze_ok", "sz_ok"))
        b_full, b_free, c_full, cs_ok = (sem(n) for n in ("b_full", "b_free", "c_full", "cs_ok"))
        dA_zero, dA_ok, scan_ok, hc_ok, red_ok = (sem(n) for n in ("dA_zero", "dA_ok", "scan_ok", "hc_ok", "red_ok"))
        yd_ok, yz_ok, x1_ok = (sem(n) for n in ("yd_ok", "yz_ok", "x1_ok"))
        fmv_ok, frs_ok, finv_ok, xqm_ok, xqT_ok = (
            sem(n) for n in ("fmv_ok", "frs_ok", "finv_ok", "xqm_ok", "xqT_ok"))
        gg_ok, gw_ok, ssq_ok = (sem(n) for n in ("gg_ok", "gw_ok", "ssq_ok"))
        gv_ok, grs_ok, iq_ok = (
            sem(n) for n in ("gv_ok", "grs_ok", "iq_ok"))
        stored = [sem("stored0"), sem("stored1")]
        whi_ok, wmid_ok, wlo_ok = (sem(n) for n in ("whi_ok", "wmid_ok", "wlo_ok"))

        block = ctx.enter_context(nc.Block())

        def bank(name, b, i, n=0):
            return w_ps[:, WORK_AT[(name, b, i, n)] % NWORK, :]

        def full(name, b, i, n=0):
            return WORK_AT[(name, b, i, n)] + 1

        def emptied(name, b, i, n=0):
            return WORK_BY[WORK_AT[(name, b, i, n)]][1]

        def wp_cols(i):
            if i < 6:
                kh, c0 = i // 3, (i % 3) * BANK
                n = min(BANK, 2 * HID - c0)
                return n, [w13T[:, s, kh, c0:c0 + n] for s in range(3)]
            c0 = (i - 6) * BANK
            return BANK, [w2T[:, s, c0:c0 + BANK] for s in range(3)]

        def products(eng, E, name, b, i):
            p = b % 2
            if name == "u":
                eng.wait_ge(sig_ok, b + 1)
                if b >= 2:
                    eng.wait_ge(yd_ok, HALVES * (b - 1))
                E.tensor_tensor(u[:, p], xc[:, p], sg[:, p], ALU.mult).then_inc(u_ok, 1)
            elif name == "du":
                eng.wait_ge(dt_ok, b + 1)
                E.tensor_tensor(du[:, p], dt[:, p], u[:, p], ALU.mult).then_inc(du_ok, 1)
            elif name == "yz":
                eng.wait_ge(sz_ok, b + 1)
                eng.wait_ge(yd_ok, HALVES * (b + 1))
                E.tensor_tensor(yd[:, p], yd[:, p], ze[:, p], ALU.mult).then_inc(yz_ok, 1)
            elif name == "gated":
                t = HALVES * b + i
                eng.wait_ge(free["dve"], emptied("up", b, 2 * i + 1, 1))
                E.tensor_tensor(gg[:, i], gg[:, i], ru[:, i, 0:HID], ALU.mult).then_inc(gg_ok, 1)
                eng.wait_ge(gg_ok, t + 1)
                if t == 0:
                    eng.wait_ge(l_nw, 16)
                E.tensor_tensor(gw[:, i], gg[:, i], normw[:, :], ALU.mult).then_inc(gw_ok, 1)

        @block.sync
        def _(sp):
            ctx_v = a["ctx_1024"].rearrange("b (h p) d -> p (b h) d", p=P)
            x_v = a["x"].rearrange("b (h p) l -> p b h l", p=P)
            xp = a["L0_xattn_x_proj_w"]
            sp.dma_start(ctx_in[:, 0:HALVES, :], ctx_v[:, 0:HALVES, :]).then_inc(l_ctx0, 16)
            sp.dma_start(win_in[:, :, :], a["L0_xattn_in_proj_w"].rearrange("(h p) d -> p h d", p=P)).then_inc(l_win, 16)
            sp.wait_ge(pool_k, 3)
            sp.dma_start(xpw_in[0:RANK, :], xp[0:RANK, :]).then_inc(l_win, 16)
            for r in range(1, 4):
                sp.dma_start(xpw_in[32 * r:32 * r + 2 * NS, :], xp[RANK:RANK + 2 * NS, :]).then_inc(l_win, 16)
            sp.dma_start(dtw_in[:, :, :], a["L0_xattn_dt_proj_w"].rearrange("(h p) r -> p h r", p=P)).then_inc(l_win, 16)
            sp.dma_start(convw[:, :, :], a["L0_xattn_conv_w"].rearrange("(h p) o k -> p h (o k)", p=P)).then_inc(l_small, 16)
            with nc.allow_non_contiguous_dma("one column of channels per half"):
                for t, n in ((convb, "conv_b"), (dtb, "dt_proj_b")):
                    sp.dma_start(t[:, :], a["L0_xattn_" + n].rearrange("(h p) -> p h", p=P)).then_inc(l_small, 16)
            sp.dma_start(nega[:, :, :], a["L0_xattn_A_log"].rearrange("(h p) n -> p h n", p=P)).then_inc(l_small, 16)
            sp.dma_start(w13_in[:, :, :], a["L0_ffn_w13"].rearrange("(t p) d -> p t d", p=P)).then_inc(l_w13, 16)
            sp.dma_start(w2_in[:, :, 0:HID], a["L0_ffn_w2"].rearrange("(h p) f -> p h f", p=P)).then_inc(l_w2, 16)
            sp.dma_start(ctx_in[:, HALVES:, :], ctx_v[:, HALVES:, :]).then_inc(l_ctx, 16)
            sp.dma_start(x[:, :], x_v).then_inc(l_x, 16)
            for i, n in enumerate(("g_xattn", "g_ffn")):
                sp.dma_start(gtmp[:, i:i + 1], a[n].unsqueeze(0).broadcast_to([P, 1])).then_inc(l_g, 16)
            with nc.allow_non_contiguous_dma("one column of channels per half"):
                sp.dma_start(dskip[:, :], a["L0_xattn_D"].rearrange("(h p) -> p h", p=P)).then_inc(l_g, 16)
            sp.dma_start(normw[:, :], a["L0_ffn_norm_w"].unsqueeze(0).broadcast_to([P, HID])).then_inc(l_nw, 16)
            out_v = out.rearrange("b (h p) d -> b h p d", p=P)
            for t in range(BATCH * HALVES):
                sp.wait_ge(free["dve"], emptied("down", t // HALVES, t % HALVES))
                sp.dma_start(out_v[t // HALVES, t % HALVES], fin[:, t % 2, :]).then_inc(stored[t % 2], 16)
            for t in range(2):
                sp.wait_ge(stored[t], 16 * BATCH * HALVES // 2)

        @block.gpsimd
        def _(pool):
            n = [0]

            def link(ins):
                n[0] += 1
                ins.then_inc(pool_c, 1)
                pool.wait_ge(pool_c, n[0])

            nc.gpsimd.memset(identf[:, :], 0.0).then_inc(pool_k, 1)
            nc.gpsimd.memset(pick[:, :], 0.0).then_inc(pool_k, 1)
            nc.gpsimd.memset(xpw_in[:, :], 0.0).then_inc(pool_k, 1)
            nc.gpsimd.memset(lnsmall[:, :], SMALL)
            pool.wait_ge(pool_k, 3)
            nc.gpsimd.affine_select(out=identf[:, :], in_=identf[:, :], compare_op=ALU.not_equal, fill=1.0, base=0,
                                    pattern=[[-1, P]], channel_multiplier=1).then_inc(pool_k, 1)
            for r in range(1, 4):
                link(nc.gpsimd.affine_select(out=pick[:, :], in_=pick[:, :], compare_op=ALU.not_equal, fill=1.0,
                                             base=-32 * r, pattern=[[-1, 2 * NS]], channel_multiplier=1))
            nc.gpsimd.memset(w2_in[:, :, HID:HPAD], 0.0).then_inc(pool_k, 1)
            nc.gpsimd.memset(dA[:, :, :, :, 0:1], 0.0).then_inc(dA_zero, 1)

            for name, b, i in ORDER["pool"]:
                p = b % 2
                k = b * NG + i
                if name in ("u", "du", "yz", "gated"):
                    products(pool, nc.gpsimd, name, b, i)
                elif name == "sz":
                    pool.wait_ge(ze_ok, b + 1)
                    nc.gpsimd.tensor_tensor(ze[:, p], zn[:, p], ze[:, p], ALU.mult).then_inc(sz_ok, 1)
                elif name in ("out0", "out1"):
                    h = int(name[-1])
                    if h == 0:
                        pool.wait_ge(cs_ok, 2 * (k + 1))
                    pool.wait_ge(scan_ok, HALVES * k + h + 1)
                    nc.gpsimd.tensor_tensor(hb[:, k % 3, h], hb[:, k % 3, h], cs[:, k % 2], ALU.mult).then_inc(hc_ok, 1)
                elif name == "w_lo":
                    n_, parts = wp_cols(i)
                    pool.wait_ge(wmid_ok, i + 1)
                    nc.gpsimd.tensor_tensor(parts[2], wres[:, i % 3, 0:n_], parts[1], ALU.subtract).then_inc(wlo_ok, 1)

        @block.scalar
        def _(act):
            n = [0]
            act_fn = nc.scalar.activation

            def link(ins):
                n[0] += 1
                ins.then_inc(act_k, 1)
                act.wait_ge(act_k, n[0])

            nc.scalar.preload_act_table_set("natural_log_exp_and_others")
            act.wait_ge(pool_k, 5)

            act_fn(lnsmall[:, :], lnsmall[:, :], ACT.Ln, bias=1.0).then_inc(lns_ok, 1)

            for name, b, i in ORDER["act"]:
                p = b % 2
                k = b * NG + i
                if name == "setup":
                    act.wait_ge(work_full, full("setup", 0, 0, 0))
                    act_fn(winT[:, :], bank("setup", 0, 0, 0)[:, 0:DI], ACT.Copy).then_inc(free["act"], 1)
                    act.wait_ge(work_full, full("setup", 0, 0, 1))
                    act_fn(xpwT[:, :, :].rearrange("p h m -> p (h m)"), bank("setup", 0, 0, 1)[:, 0:DI],
                           ACT.Copy).then_inc(free["act"], 1)
                    act.wait_ge(l_small, 64)
                    link(act_fn(nega[:, :, :], nega[:, :, :], ACT.Exp))
                    act_fn(nega[:, :, :], nega[:, :, :], ACT.Copy, scale=-1.0).then_inc(nega_ok, 1)
                elif name == "sel":
                    act_fn(sel[:, :, :], pick[:, :].unsqueeze(2).broadcast_to([P, 2 * NS, P]), ACT.Copy).then_inc(sel_ok, 1)
                elif name == "ctxT":
                    act.wait_ge(work_full, full("ctxT", b, i))
                    act_fn(ctxT[:, p], bank("ctxT", b, i)[:, 0:L], ACT.Copy).then_inc(free["act"], 1)
                elif name == "sigm0":
                    act.wait_ge(free["dve"], emptied("inproj", b, i))
                    act_fn(sg[:, p], xc[:, p], ACT.Exp, scale=-1.0).then_inc(conv_e, 1)
                elif name == "sigm1":
                    act.wait_ge(clamp_ok, b + 1)
                    link(act_fn(sg[:, p], sg[:, p], ACT.Ln, bias=1.0))
                    act_fn(sg[:, p], sg[:, p], ACT.Exp, scale=-1.0).then_inc(sig_ok, 1)
                elif name == "absx":
                    act.wait_ge(work_full, full("dtproj", b, i))
                    d_ps = bank("dtproj", b, i).rearrange("p (h l) -> p h l", h=HALVES)
                    for h in range(HALVES):
                        last = act_fn(q[:, p, h], d_ps[:, h], ACT.Abs, bias=dtb[:, h:h + 1])
                    last.then_inc(abs_ok, 1)
                    for h in range(HALVES):
                        last = act_fn(xs[:, p, h], d_ps[:, h], ACT.Relu, bias=dtb[:, h:h + 1])
                    last.then_inc(free["act"], 1)
                    act.wait_ge(abs_ok, b + 1)
                    act_fn(q[:, p], q[:, p], ACT.Exp, scale=-1.0).then_inc(q_ok, 1)
                elif name == "ln1q":
                    act.wait_ge(ql_ok, b + 1)
                    act_fn(lw[:, p], lw[:, p], ACT.Ln, bias=1.0).then_inc(lw_ok, 1)
                elif name == "xrs":
                    act.wait_ge(xmv_ok, 1)
                    link(act_fn(xrs[:, :], xt1[:, :], ACT.Ln))
                    act_fn(xrs[:, :], xrs[:, :], ACT.Exp, scale=-0.5).then_inc(xrs_ok, 1)
                    act.wait_ge(l_g, 48)
                    act_fn(gates[:, :], gtmp[:, :], ACT.Exp, scale=2.0).then_inc(gexp_ok, 1)
                elif name == "zsig":
                    act.wait_ge(zn_ok, HALVES * (b + 1))
                    if b >= 2:
                        act.wait_ge(yz_ok, b - 1)
                    link(act_fn(ze[:, p], zn[:, p], ACT.Exp, scale=-1.0))
                    link(act_fn(ze[:, p], ze[:, p], ACT.Ln, bias=1.0))
                    act_fn(ze[:, p], ze[:, p], ACT.Exp, scale=-1.0).then_inc(ze_ok, 1)
                elif name in ("decay0", "decay1"):
                    h = int(name[-1])
                    act.wait_ge(dt_ok, b + 1)
                    if k == 0 and h == 0:
                        act.wait_ge(nega_ok, 1)
                    if k >= 2:
                        act.wait_ge(scan_ok, HALVES * (k - 2) + h + 1)
                    for s in range(GN):
                        last = act_fn(dA[:, k % 2, h, s, 1:L], dt[:, p, h, 1:L], ACT.Exp,
                                      scale=nega[:, h, GN * i + s:GN * i + s + 1])
                    last.then_inc(dA_ok, 1)
                elif name == "c_copy":
                    if k >= 2:
                        act.wait_ge(hc_ok, HALVES * (k - 1))
                    for c in range(2):
                        act.wait_ge(c_full, 2 * k + c + 1)
                        act_fn(cs[:, k % 2, c * BANK:(c + 1) * BANK], c_ps[:, c, :], ACT.Copy).then_inc(cs_ok, 1)
                elif name == "rs1":
                    act.wait_ge(fmv_ok, b + 1)
                    link(act_fn(frs[:, :], fs[:, :], ACT.Ln))
                    act_fn(frs[:, :], frs[:, :], ACT.Exp, scale=-0.5).then_inc(frs_ok, 1)
                elif name == "xqT":
                    act.wait_ge(work_full, full("xqT", b, i))
                    act_fn(xqT[:, :, :, :].rearrange("p k h t -> p (k h t)"), bank("xqT", b, i), ACT.Copy,
                           bias=-MAGIC).then_inc(free["act"], 1)
                elif name == "relu":
                    h, c = i // 2, i % 2
                    act.wait_ge(work_full, full("up", b, i, 0))
                    act_fn(ru[:, h, c * UC:(c + 1) * UC], bank("up", b, i, 0)[:, 0:UC], ACT.Relu,
                           scale=finv[:, h:h + 1]).then_inc(free["act"], 1)
                elif name == "square":
                    act.wait_ge(gw_ok, HALVES * b + i + 1)
                    act_fn(gg[:, i], gg[:, i], ACT.Square, accum_out=ssq[:, i:i + 1]).then_inc(ssq_ok, 1)
                elif name == "rs2":
                    act.wait_ge(gv_ok, b + 1 + i)
                    hs = slice(i, i + 1) if b == BATCH - 1 else slice(0, HALVES)
                    link(act_fn(grs[:, hs], gv[:, hs], ACT.Ln))
                    act_fn(grs[:, hs], grs[:, hs], ACT.Exp, scale=-0.5).then_inc(grs_ok, 1)
                elif name == "iqT":
                    for c in range(2):
                        act.wait_ge(work_full, full("iqT", b, i, c))
                        act_fn(iqT[:, i, 3 * c:3 * c + 3, :].rearrange("p f t -> p (f t)"),
                               bank("iqT", b, i, c)[:, 0:3 * P], ACT.Copy, bias=-MAGIC).then_inc(free["act"], 1)
                elif name == "w_hi":
                    n_, parts = wp_cols(i)
                    act.wait_ge(work_full, full("w", 0, i))
                    act_fn(parts[0], bank("w", 0, i)[:, 0:n_], ACT.Copy).then_inc(whi_ok, 1)
                elif name == "w_mid":
                    n_, parts = wp_cols(i)
                    act.wait_ge(free["dve"], emptied("w", 0, i))
                    act_fn(parts[1], wres[:, i % 3, 0:n_], ACT.Copy).then_inc(wmid_ok, 1)

        @block.vector
        def _(dve):
            V = nc.vector
            n = [0]

            def link(ins):
                n[0] += 1
                ins.then_inc(dve_k, 1)
                dve.wait_ge(dve_k, n[0])

            def mark(ins):
                n[0] += 1
                ins.then_inc(dve_k, 1)
                return n[0]

            def newton(y, v, t):
                link(V.tensor_tensor(t, y, y, ALU.mult))
                link(V.tensor_tensor(t, t, v, ALU.mult))
                link(V.tensor_scalar(t, t, -0.5, 1.5, ALU.mult, ALU.add))
                link(V.tensor_tensor(y, y, t, ALU.mult))

            for name, b, i in ORDER["dve"]:
                p = b % 2
                k = b * NG + i
                if name in ("u", "du", "yz", "gated"):
                    products(dve, V, name, b, i)
                elif name == "setup":
                    dve.wait_ge(work_full, full("setup", 0, 0, 2))
                    V.tensor_copy(dtwT[:, :], bank("setup", 0, 0, 2)[0:RANK, 0:DI]).then_inc(free["dve"], 1)
                elif name == "conv":
                    dve.wait_ge(work_full, full("inproj", b, i))
                    if b == 0:
                        dve.wait_ge(l_small, 64)
                    h_ps = bank("inproj", b, i).rearrange("p (h l) -> p h l", h=HALVES)
                    at = [0] * HALVES
                    for h in range(HALVES):
                        at[h] = mark(V.tensor_scalar(xc[:, p, h], h_ps[:, h], convw[:, h, TAPS - 1:TAPS],
                                                     convb[:, h:h + 1], ALU.mult, ALU.add))
                    for s in range(1, TAPS):
                        for h in range(HALVES):
                            dve.wait_ge(dve_k, at[h])
                            last = V.scalar_tensor_tensor(
                                out=xc[:, p, h, s:L], in0=h_ps[:, h, 0:L - s], scalar=convw[:, h, TAPS - 1 - s:TAPS - s],
                                in1=xc[:, p, h, s:L], op0=ALU.mult, op1=ALU.add)
                            if s < TAPS - 1 or h == 0:
                                at[h] = mark(last)
                    last.then_inc(free["dve"], 1)
                elif name == "clamp":
                    dve.wait_ge(conv_e, b + 1)
                    V.tensor_scalar(sg[:, p], sg[:, p], CLAMP, None, ALU.min).then_inc(clamp_ok, 1)
                elif name == "split":
                    x_ps = bank("xdbl", b, i)[:, 0:L]
                    dve.wait_ge(work_full, full("xdbl", b, i))
                    V.tensor_copy(dtlow[:, p], x_ps[0:RANK, :]).then_inc(dtlow_ok, 1)
                    link(V.tensor_copy(bcs[:, p], x_ps))
                    V.tensor_tensor(bcr[:, p], x_ps, bcs[:, p], ALU.subtract).then_inc(free["dve"], 1)
                    dve.wait_ge(free["dve"], emptied("xdbl", b, i))
                    link(V.tensor_copy(bcs[64:P, p], bcr[64:P, p]))
                    V.tensor_tensor(bcs[96:P, p], bcr[96:P, p], bcs[96:P, p], ALU.subtract).then_inc(bcs_ok, 1)
                elif name == "series":
                    dve.wait_ge(q_ok, b + 1)
                    V.tensor_scalar(lw[:, p], q[:, p], SMALL, None, ALU.max).then_inc(ql_ok, 1)
                    dve.wait_ge(ql_ok, b + 1)
                    link(V.tensor_scalar(q[:, p], q[:, p], SMALL, None, ALU.min))
                    link(V.tensor_scalar(rr[:, p], q[:, p], 1.0 / 3.0, -0.5, ALU.mult, ALU.add))
                    link(V.tensor_tensor(rr[:, p], rr[:, p], q[:, p], ALU.mult))
                    link(V.scalar_tensor_tensor(out=q[:, p], in0=rr[:, p], scalar=1.0, in1=q[:, p],
                                                op0=ALU.add, op1=ALU.mult))
                elif name == "dt":
                    dve.wait_ge(lw_ok, b + 1)
                    if b == 0:
                        dve.wait_ge(lns_ok, 1)
                    link(V.scalar_tensor_tensor(out=lw[:, p], in0=lw[:, p], scalar=lnsmall[:, 0:1], in1=q[:, p],
                                                op0=ALU.subtract, op1=ALU.add))
                    dve.wait_ge(free["act"], emptied("dtproj", b, i))
                    V.tensor_tensor(dt[:, p], xs[:, p], lw[:, p], ALU.add).then_inc(dt_ok, 1)
                elif name == "xstat":
                    dve.wait_ge(l_x, 16)
                    for j in range(BATCH * HALVES):
                        at = mark(V.bn_stats(xstat[:, j], x[:, j // HALVES, j % HALVES]))
                    dve.wait_ge(dve_k, at)
                    for j in range(BATCH * HALVES):
                        at = mark(V.bn_aggr(xmv[:, j], xstat[:, j]))
                    dve.wait_ge(dve_k, at)
                    V.tensor_scalar(xt1[:, :], xmv[:, :, 1], EPS, None, ALU.add).then_inc(xmv_ok, 1)
                elif name == "gates":
                    dve.wait_ge(xrs_ok, 1)
                    newton(xrs[:, :], xt1[:, :], xstat[:, :, 0])
                    dve.wait_ge(gexp_ok, 1)
                    link(V.tensor_scalar(gates[:, :], gates[:, :], 1.0, None, ALU.add))
                    link(V.reciprocal(gates[:, :], gates[:, :]))
                    link(V.tensor_scalar(gates[:, :], gates[:, :], -2.0, 1.0, ALU.mult, ALU.add))
                elif name == "z":
                    if b >= 2:
                        dve.wait_ge(sz_ok, b - 1)
                    for h in range(HALVES):
                        j = HALVES * b + h
                        V.tensor_scalar(zn[:, p, h], x[:, b, h], xmv[:, j, 0:1], xrs[:, j:j + 1],
                                        ALU.subtract, ALU.mult).then_inc(zn_ok, 1)
                elif name in ("mix0", "mix1"):
                    h = int(name[-1])
                    if h == 0:
                        dve.wait_ge(du_ok, b + 1)
                        dve.wait_ge(b_full, k + 1)
                    if k >= 3:
                        dve.wait_ge(red_ok, HALVES * (k - 3) + h + 1)
                    V.tensor_tensor(hb[:, k % 3, h].rearrange("p (n l) -> p n l", n=GN),
                                    b_ps[:, :, :].rearrange("p c (n l) -> p (c n) l", l=L),
                                    du[:, p, h].unsqueeze(1).broadcast_to([P, GN, L]), ALU.mult).then_inc(b_free, 1)
                elif name in ("scan0", "scan1"):
                    h = int(name[-1])
                    if k == 0:
                        dve.wait_ge(dA_zero, 1)
                    dve.wait_ge(dA_ok, HALVES * k + h + 1)
                    dve.wait_ge(b_free, HALVES * k + h + 1)
                    V.tensor_tensor_scan(hb[:, k % 3, h], dA[:, k % 2, h].rearrange("p n l -> p (n l)"),
                                         hb[:, k % 3, h], 0.0, ALU.mult, ALU.add).then_inc(scan_ok, 1)
                elif name == "yd":
                    dve.wait_ge(red_ok, HALVES * NG * (b + 1))
                    for h in range(HALVES):
                        V.scalar_tensor_tensor(out=yd[:, p, h], in0=u[:, p, h], scalar=dskip[:, h:h + 1],
                                               in1=y_ps[:, h], op0=ALU.mult, op1=ALU.add).then_inc(yd_ok, 1)
                elif name == "x1":
                    dve.wait_ge(work_full, full("yT", b, i))
                    xb = x[:, b].rearrange("p h l -> p (h l)")
                    V.scalar_tensor_tensor(out=xb, in0=bank("yT", b, i), scalar=gates[:, 0:1], in1=xb,
                                           op0=ALU.mult, op1=ALU.add).then_inc(free["dve"], 1)
                    dve.wait_ge(free["dve"], emptied("yT", b, i))
                    for h in range(HALVES):
                        at = mark(V.bn_stats(fstat[:, h], x[:, b, h]))
                    dve.wait_ge(dve_k, at)
                    for h in range(HALVES):
                        at = mark(V.bn_aggr(fmv[:, h], fstat[:, h]))
                    dve.wait_ge(dve_k, at)
                    V.tensor_scalar(fs[:, :], fmv[:, :, 1], EPS, None, ALU.add).then_inc(fmv_ok, 1)
                    for h in range(HALVES):
                        at = mark(V.tensor_scalar(xn[:, h], x[:, b, h], fmv[:, h, 0:1], None, ALU.subtract))
                    dve.wait_ge(dve_k, at)
                    famx = mark(V.tensor_reduce(fam[:, :], xn[:, :, :], AX.X, ALU.max, apply_absolute_value=True))
                elif name == "quant1":
                    dve.wait_ge(frs_ok, b + 1)
                    dve.wait_ge(dve_k, famx)
                    link(V.tensor_tensor(fam[:, :], fam[:, :], frs[:, :], ALU.mult))
                    link(V.tensor_scalar(fam[:, :], fam[:, :], 1e-5, None, ALU.max))
                    link(V.reciprocal(fs[:, :], fam[:, :]))
                    V.tensor_scalar(finv[:, :], fam[:, :], 1.0 / 127.0, None, ALU.mult).then_inc(finv_ok, 1)
                    link(V.scalar_tensor_tensor(out=fs[:, :], in0=fs[:, :], scalar=127.0, in1=frs[:, :],
                                                op0=ALU.mult, op1=ALU.mult))
                    for h in range(HALVES):
                        V.tensor_scalar(xn[:, h], xn[:, h], fs[:, h:h + 1], MAGIC, ALU.mult, ALU.add).then_inc(xqm_ok, 1)
                elif name == "gate":
                    h, c = i // 2, i % 2
                    dve.wait_ge(work_full, full("up", b, i, 1))
                    dve.wait_ge(free["act"], emptied("up", b, i, 0))
                    V.scalar_tensor_tensor(out=gg[:, h, c * UC:(c + 1) * UC], in0=bank("up", b, i, 1)[:, 0:UC],
                                           scalar=finv[:, h:h + 1], in1=ru[:, h, c * UC:(c + 1) * UC],
                                           op0=ALU.mult, op1=ALU.mult).then_inc(free["dve"], 1)
                elif name == "absmax":
                    dve.wait_ge(gw_ok, HALVES * b + i + 1)
                    at = mark(V.tensor_reduce(gam[:, i:i + 1], gw[:, i], AX.X, ALU.max, apply_absolute_value=True))
                    if b == BATCH - 1 or i == HALVES - 1:
                        hs = slice(i, i + 1) if b == BATCH - 1 else slice(0, HALVES)
                        dve.wait_ge(ssq_ok, HALVES * b + i + 1)
                        V.tensor_scalar(gv[:, hs], ssq[:, hs], 1.0 / HID, EPS, ALU.mult, ALU.add).then_inc(gv_ok, 1)
                elif name == "scale2":
                    hs = slice(i, i + 1) if b == BATCH - 1 else slice(0, HALVES)
                    dve.wait_ge(grs_ok, b + 1 + i)
                    newton(grs[:, hs], gv[:, hs], gt[:, hs])
                    link(V.tensor_tensor(gt[:, hs], gam[:, hs], grs[:, hs], ALU.mult))
                    link(V.tensor_scalar(gt[:, hs], gt[:, hs], 1e-5, None, ALU.max))
                    link(V.reciprocal(gc[:, hs], gt[:, hs]))
                    at = mark(V.tensor_scalar(gos[:, b, hs], gt[:, hs], gates[:, 1:2], 1.0 / 127.0, ALU.mult, ALU.mult))
                    link(V.scalar_tensor_tensor(out=gc[:, hs], in0=gc[:, hs], scalar=127.0, in1=grs[:, hs],
                                                op0=ALU.mult, op1=ALU.mult))
                    if b == 0:
                        link(V.memset(ru[:, :, HID:HPAD], MAGIC))
                elif name == "quant2":
                    V.tensor_scalar(ru[:, i, 0:HID], gw[:, i], gc[:, i:i + 1], MAGIC, ALU.mult, ALU.add).then_inc(iq_ok, 1)
                elif name == "final":
                    t = HALVES * b + i
                    dve.wait_ge(work_full, full("down", b, i))
                    if t >= 2:
                        dve.wait_ge(stored[t % 2], 16 * (t // 2))
                    V.scalar_tensor_tensor(out=fin[:, t % 2], in0=bank("down", b, i)[:, 0:L], scalar=gos[:, b, i:i + 1],
                                           in1=x[:, b, i], op0=ALU.mult, op1=ALU.add).then_inc(free["dve"], 1)
                elif name == "w_res":
                    n_, parts = wp_cols(i)
                    dve.wait_ge(whi_ok, i + 1)
                    if i >= 3:
                        dve.wait_ge(wlo_ok, i - 2)
                    V.tensor_tensor(wres[:, i % 3, 0:n_], bank("w", 0, i)[:, 0:n_], parts[0],
                                    ALU.subtract).then_inc(free["dve"], 1)

        @block.tensor
        def _(pe):
            T = nc.tensor

            def claim(name, b, i, n=0):
                w = WORK_AT[(name, b, i, n)]
                if w >= NWORK:
                    who, count = WORK_BY[w - NWORK]
                    pe.wait_ge(free[who], count)
                return bank(name, b, i, n)

            for name, b, i in ORDER["pe"]:
                p = b % 2
                k = b * NG + i
                if name == "setup":
                    pe.wait_ge(pool_k, 4)
                    pe.wait_ge(l_win, 96)
                    ps = claim("setup", 0, 0, 0)
                    for h in range(HALVES):
                        last = T.transpose(ps[:, h * P:(h + 1) * P], win_in[:, h, :], identf[:, :])
                    last.then_inc(work_full, 1)
                    ps = claim("setup", 0, 0, 1)
                    for h in range(HALVES):
                        last = T.transpose(ps[:, h * P:(h + 1) * P], xpw_in[:, h * P:(h + 1) * P], identf[:, :])
                    last.then_inc(work_full, 1)
                    ps = claim("setup", 0, 0, 2)
                    for h in range(HALVES):
                        last = T.transpose(ps[0:RANK, h * P:(h + 1) * P], dtw_in[:, h, :], identf[:, :])
                    last.then_inc(work_full, 1)
                elif name == "ctxT":
                    pe.wait_ge(l_ctx0 if b == 0 else l_ctx, 16)
                    ps = claim(name, b, i)
                    for h in range(HALVES):
                        last = T.transpose(ps[:, h * P:(h + 1) * P], ctx_in[:, HALVES * b + h, :], identf[:, :])
                    last.then_inc(work_full, 1)
                elif name == "inproj":
                    pe.wait_ge(free["act"], emptied("ctxT", b, i))
                    ps = claim(name, b, i)
                    for h in range(HALVES):
                        last = T.matmul(ps[:, h * L:(h + 1) * L], winT[:, h * P:(h + 1) * P], ctxT[:, p], start=True, stop=True)
                    last.then_inc(work_full, 1)
                elif name == "xdbl":
                    pe.wait_ge(u_ok, b + 1)
                    ps = claim(name, b, i)
                    for h in range(HALVES):
                        last = T.matmul(ps[:, 0:L], xpwT[:, h], u[:, p, h], start=(h == 0), stop=(h == HALVES - 1))
                    last.then_inc(work_full, 1)
                elif name == "dtproj":
                    pe.wait_ge(dtlow_ok, b + 1)
                    if b == 0:
                        pe.wait_ge(free["dve"], emptied("setup", 0, 0, 2))
                    ps = claim(name, b, i)
                    for h in range(HALVES):
                        last = T.matmul(ps[:, h * L:(h + 1) * L], dtwT[:, h * P:(h + 1) * P], dtlow[:, p], start=True, stop=True)
                    last.then_inc(work_full, 1)
                elif name == "bc_b":
                    pe.wait_ge(bcs_ok, b + 1)
                    if k == 0:
                        pe.wait_ge(sel_ok, 1)
                    if k:
                        pe.wait_ge(b_free, HALVES * k)
                    for c in range(2):
                        for s in range(2):
                            last = T.matmul(b_ps[:, c, s * L:(s + 1) * L], sel[:, GN * i + 2 * c + s], bcs[:, p],
                                            start=True, stop=True)
                    last.then_inc(b_full, 1)
                elif name == "bc_c":
                    for c in range(2):
                        if k:
                            pe.wait_ge(cs_ok, 2 * (k - 1) + c + 1)
                        for s in range(2):
                            last = T.matmul(c_ps[:, c, s * L:(s + 1) * L], sel[:, NS + GN * i + 2 * c + s], bcs[:, p],
                                            start=True, stop=True)
                        last.then_inc(c_full, 1)
                elif name in ("sum0", "sum1"):
                    h = int(name[-1])
                    if i == 0 and h == 0 and b:
                        pe.wait_ge(yd_ok, HALVES * b)
                    pe.wait_ge(hc_ok, HALVES * k + h + 1)
                    for s in range(GN):
                        last = T.matmul(y_ps[:, h], identf[:, :], hb[:, k % 3, h, s * L:(s + 1) * L],
                                        start=(i == 0 and s == 0 and h == 0), stop=(i == NG - 1 and s == GN - 1),
                                        skip_group_check=True)
                    last.then_inc(red_ok, 1)
                elif name == "yT":
                    pe.wait_ge(yz_ok, b + 1)
                    ps = claim(name, b, i)
                    for t in range(HALVES):
                        for h in range(HALVES):
                            last = T.transpose(ps[:, t * DI + h * P:t * DI + (h + 1) * P], yd[:, p, h, t * P:(t + 1) * P],
                                               identf[:, :])
                    last.then_inc(work_full, 1)
                elif name == "xqT":
                    pe.wait_ge(xqm_ok, HALVES * (b + 1))
                    ps = claim(name, b, i)
                    for kh in range(HALVES):
                        for h in range(HALVES):
                            c = (kh * HALVES + h) * P
                            last = T.transpose(ps[:, c:c + P], xn[:, h, kh * P:(kh + 1) * P], identf[:, :])
                    last.then_inc(work_full, 1)
                elif name == "up":
                    h, c = i // 2, i % 2
                    pe.wait_ge(free["act"], emptied("xqT", b, 0))
                    if b == 0 and i == 0:
                        pe.wait_ge(wlo_ok, NWP)
                    for j in range(2):
                        ps = claim(name, b, i, j)
                        c0 = j * HID + c * UC
                        for kh in range(HALVES):
                            for s in range(3):
                                last = T.matmul(ps[:, 0:UC], xqT[:, kh, h, :], w13T[:, s, kh, c0:c0 + UC],
                                                start=(kh == 0 and s == 0), stop=(kh == 1 and s == 2))
                        last.then_inc(work_full, 1)
                elif name == "iqT":
                    pe.wait_ge(iq_ok, HALVES * b + i + 1)
                    for c in range(2):
                        ps = claim(name, b, i, c)
                        for f in range(3):
                            last = T.transpose(ps[:, f * P:(f + 1) * P], ru[:, i, (3 * c + f) * P:(3 * c + f + 1) * P],
                                               identf[:, :])
                        last.then_inc(work_full, 1)
                elif name == "down":
                    ps = claim(name, b, i)
                    pe.wait_ge(free["act"], emptied("iqT", b, i, 1))
                    for f in range(FB):
                        for s in range(3):
                            last = T.matmul(ps[:, 0:DI], iqT[:, i, f, :], w2T[:, s, f * DI:(f + 1) * DI],
                                            start=(f == 0 and s == 0), stop=(f == FB - 1 and s == 2))
                    last.then_inc(work_full, 1)
                elif name == "w":
                    ps = claim(name, b, i)
                    if i < 6:
                        pe.wait_ge(l_w13, 16)
                        kh, t0 = i // 3, (i % 3) * 4
                        for t in range(t0, min(t0 + 4, 11)):
                            last = T.transpose(ps[:, (t - t0) * P:(t - t0 + 1) * P], w13_in[:, t, kh * P:(kh + 1) * P],
                                               identf[:, :])
                    else:
                        pe.wait_ge(l_w2, 16)
                        pe.wait_ge(pool_k, 5)
                        for j in range(4):
                            f, h = 2 * (i - 6) + j // 2, j % 2
                            last = T.transpose(ps[:, j * P:(j + 1) * P], w2_in[:, h, f * P:(f + 1) * P], identf[:, :])
                    last.then_inc(work_full, 1)


def kernel(**inputs):
    import numpy as np
    import concourse.bacc as bacc
    from concourse.bass_utils import run_bass_kernel_spmd

    nc = bacc.Bacc("TRN2", target_bir_lowering=False, num_devices=1)
    arrays, args = {}, {}
    for name, v in inputs.items():
        v = np.ascontiguousarray(v)
        arrays["in_" + name] = v
        args[name] = nc.dram_tensor("in_" + name, v.shape, mybir.dt.from_np(v.dtype), kind="ExternalInput").ap()
    out = nc.dram_tensor("out", (BATCH, L, DI), fp32, kind="ExternalOutput").ap()
    build(nc, args, out)
    r = run_bass_kernel_spmd(nc, [arrays], core_ids=[0])
    return r.results[0]["out"]
```

```python
import concourse.bass as bass
from concourse import mybir
from contextlib import ExitStack

fp32 = mybir.dt.float32
bf16 = mybir.dt.bfloat16
ALU = mybir.AluOpType
ACT = mybir.ActivationFunctionType
AX = mybir.AxisListType

P = 128
BATCH, L, DI = 4, 256, 256
DM = 128
NS, RANK, TAPS = 16, 8, 4
HALVES = DI // P
GN = 4
NG = NS // GN
HID = 704
HPAD = 768
FB = HPAD // P
UC = HID // 2
EPS = 1e-5
MAGIC = 1.5 * 2.0 ** 23
SMALL = 2.0 ** -8
CLAMP = 2.0 ** 60
BANK = 512
NWORK = 3
NWP = 9

GT = 4
TICKS = GT * NG
CORE = [
    ("decay0", "act", -0.5), ("bc_b", "pe", 0), ("decay1", "act", 0), ("bc_c", "pe", 0.5), ("mix0", "dve", 0.5),
    ("mix1", "dve", 0.5), ("c_copy", "act", 1), ("scan0", "dve", 1), ("scan1", "dve", 2.5), ("out0", "pool", 3),
    ("out1", "pool", 3), ("sum0", "pe", 6), ("sum1", "pe", 6.5),
]


def tiles(b, i):
    return range(i, i + 1) if b == BATCH - 1 else range(HALVES)


def group(b, i):
    if b == BATCH - 1:
        return P * (i // 2), P, 2 * GN * (i % 2), 2 * GN
    return 0, L, GN * i, GN


ONCE = [
    ("setup", 0, "pe", -100), ("setup", 0, "act", -100), ("setup", 0, "dve", -100), ("w_lo", 0, "pool", -16.5),
    ("sel", 0, "act", -16), ("w_lo", 1, "pool", -13.5), ("w", 0, "pe", -11), ("w_res", 0, "dve", -10.5),
    ("w_hi", 0, "act", -10), ("w", 1, "pe", -10), ("w_lo", 2, "pool", -10), ("w_hi", 1, "act", -8.5),
    ("w_mid", 0, "act", -7.5), ("w_res", 1, "dve", -7.5), ("w_hi", 2, "act", -6), ("xstat", 0, "dve", -5.5),
    ("w_hi", 3, "act", -5.5), ("w_hi", 4, "act", -5.5), ("w", 2, "pe", -5), ("w_lo", 3, "pool", -5),
    ("w_mid", 1, "act", -4.5), ("w_res", 2, "dve", -4.5), ("w_res", 3, "dve", -4.5), ("w_res", 4, "dve", -4.5),
    ("w_mid", 2, "act", -4), ("w", 3, "pe", -4), ("w_mid", 3, "act", -4), ("w_hi", 5, "act", -4),
    ("w", 4, "pe", -3.5), ("xrs", 0, "act", -3), ("w_mid", 4, "act", -3), ("w_hi", 6, "act", -3),
    ("w_lo", 4, "pool", -2.5), ("w_res", 5, "dve", -2), ("w_lo", 5, "pool", -2), ("w", 5, "pe", -1.5),
    ("w_mid", 5, "act", -1), ("w_lo", 6, "pool", -1), ("w_res", 6, "dve", 0.5), ("w_mid", 6, "act", 0.5),
    ("w_hi", 7, "act", 0.5), ("w_res", 7, "dve", 1), ("w", 6, "pe", 1.5), ("gates", 0, "dve", 2), ("w", 7, "pe", 2.5),
    ("w_mid", 7, "act", 3), ("w", 8, "pe", 3), ("w_hi", 8, "act", 7.5), ("w_lo", 7, "pool", 8),
    ("w_res", 8, "dve", 9), ("w_mid", 8, "act", 11.5), ("w_lo", 8, "pool", 12),
]
FIRST = [
    ("ctxT", 0, "pe", -35), ("ctxT", 0, "act", -16.5), ("conv", 0, "dve", -16.5), ("sigm0", 0, "act", -16),
    ("inproj", 0, "pe", -14), ("sigm1", 0, "act", -13), ("clamp", 0, "dve", -12.5), ("xdbl", 0, "pe", -12.5),
    ("u", 0, "dve", -11), ("split", 0, "dve", -11), ("dtproj", 0, "pe", -8.5), ("absx", 0, "act", -6.5),
    ("ln1q", 0, "act", -5.5), ("series", 0, "dve", -5), ("dt", 0, "dve", -4), ("du", 0, "dve", -1),
    ("z", 0, "dve", 3.5), ("zsig", 0, "act", 5.5), ("sz", 0, "pool", 12), ("yz", 0, "pool", 17.5),
    ("yd", 0, "dve", 19), ("yT", 0, "pe", 20.5), ("x1", 0, "dve", 22.5), ("rs1", 0, "act", 22.5),
    ("quant1", 0, "dve", 23.5), ("xqT", 0, "pe", 24.5), ("xqT", 0, "act", 24.5), ("up", 0, "pe", 26),
    ("relu", 0, "act", 27), ("up", 1, "pe", 27.5), ("gate", 0, "dve", 28), ("relu", 1, "act", 29.5),
    ("gate", 1, "dve", 31), ("up", 2, "pe", 31.5), ("relu", 2, "act", 31.5), ("gate", 2, "dve", 32.5),
    ("relu", 3, "act", 32.5), ("up", 3, "pe", 33), ("gated", 0, "pool", 33.5), ("gate", 3, "dve", 33.5),
    ("gated", 1, "pool", 33.5), ("absmax", 0, "dve", 35), ("absmax", 1, "dve", 37), ("square", 0, "act", 38),
    ("square", 1, "act", 38.5), ("rs2", 0, "act", 38.7), ("scale2", 0, "dve", 39), ("quant2", 0, "dve", 40.5),
    ("quant2", 1, "dve", 40.5), ("iqT", 0, "pe", 41), ("iqT", 1, "pe", 41), ("outscale", 0, "dve", 41.5),
    ("iqT", 0, "act", 42), ("final", 0, "dve", 42), ("down", 0, "pe", 43), ("final", 1, "dve", 43),
    ("iqT", 1, "act", 43.5), ("down", 1, "pe", 43.5),
]
MIDDLE = [
    ("ctxT", 0, "act", -22.5), ("ctxT", 0, "pe", -22), ("inproj", 0, "pe", -19), ("conv", 0, "dve", -17.5),
    ("sigm0", 0, "act", -15.5), ("clamp", 0, "dve", -14.5), ("sigm1", 0, "act", -11), ("z", 0, "dve", -10),
    ("u", 0, "pool", -9.5), ("xdbl", 0, "pe", -9.5), ("split", 0, "dve", -8), ("dtproj", 0, "pe", -7.5),
    ("absx", 0, "act", -7.5), ("series", 0, "dve", -6), ("ln1q", 0, "act", -5.5), ("dt", 0, "dve", -5.5),
    ("du", 0, "pool", -4), ("zsig", 0, "act", -3), ("sz", 0, "pool", 12.5), ("yd", 0, "dve", 20.5),
    ("yz", 0, "pool", 23), ("yT", 0, "pe", 23), ("x1", 0, "dve", 24.5), ("rs1", 0, "act", 26),
    ("quant1", 0, "dve", 26), ("xqT", 0, "pe", 28), ("xqT", 0, "act", 28), ("relu", 0, "act", 28),
    ("gate", 0, "dve", 28.5), ("up", 0, "pe", 29), ("up", 1, "pe", 29), ("relu", 1, "act", 29),
    ("gate", 1, "dve", 29), ("up", 2, "pe", 29.5), ("relu", 2, "act", 29.5), ("gate", 2, "dve", 29.5),
    ("up", 3, "pe", 29.5), ("relu", 3, "act", 29.5), ("gate", 3, "dve", 29.5), ("gated", 0, "pool", 30.5),
    ("gated", 1, "pool", 31), ("square", 0, "act", 31), ("absmax", 0, "dve", 31), ("square", 1, "act", 34),
    ("absmax", 1, "dve", 34), ("rs2", 0, "act", 35.2), ("scale2", 0, "dve", 36), ("quant2", 0, "dve", 36.5),
    ("quant2", 1, "dve", 36.5), ("iqT", 0, "pe", 37), ("outscale", 0, "dve", 38), ("iqT", 0, "act", 39.5),
    ("iqT", 1, "pe", 41), ("down", 0, "pe", 41.5), ("final", 0, "dve", 42.5), ("iqT", 1, "act", 42.5),
    ("final", 1, "dve", 42.5), ("down", 1, "pe", 43.5),
]
LAST = [
    ("ctxT", 0, "pe", -14.5), ("inproj", 0, "pe", -14), ("ctxT", 0, "act", -13.5), ("conv", 0, "dve", -13.5),
    ("sigm0", 0, "act", -10.5), ("clamp", 0, "dve", -9.5), ("u", 0, "pool", -8), ("z", 0, "dve", -8),
    ("split", 0, "dve", -6.5), ("sigm1", 0, "act", -5.5), ("xdbl", 0, "pe", -5.5), ("dtproj", 0, "pe", -5),
    ("series", 0, "dve", -5), ("zsig", 0, "act", -5), ("absx", 0, "act", -4.5), ("ln1q", 0, "act", -4.5),
    ("dt", 0, "dve", -4.5), ("du", 0, "pool", -4.5), ("edge", 0, "dve", -2), ("edge", 0, "act", 2.5),
    ("sz", 0, "pool", 9.5), ("yd", 0, "dve", 10.5), ("yz", 0, "dve", 12), ("x1", 0, "dve", 13.5), ("yT", 0, "pe", 14),
    ("rs1", 0, "act", 14), ("quant1", 0, "dve", 14), ("xqT", 0, "act", 14), ("relu", 0, "act", 14),
    ("xqT", 0, "pe", 15.5), ("up", 0, "pe", 15.5), ("gate", 0, "dve", 15.5), ("up", 1, "pe", 16),
    ("gated", 0, "pool", 16), ("gate", 1, "dve", 18.5), ("relu", 1, "act", 19), ("yd", 1, "dve", 20.5),
    ("yz", 1, "dve", 20.5), ("x1", 1, "dve", 21.5), ("quant1", 1, "dve", 22), ("yT", 1, "pe", 23.5),
    ("absmax", 0, "dve", 24.5), ("xqT", 1, "pe", 27.5), ("scale2", 0, "dve", 28.5), ("quant2", 0, "dve", 28.5),
    ("rs1", 1, "act", 28.5), ("gate", 2, "dve", 31), ("square", 0, "act", 32), ("outscale", 0, "dve", 32.5),
    ("xqT", 1, "act", 33.5), ("up", 2, "pe", 41.5), ("iqT", 0, "pe", 42), ("gate", 3, "dve", 43.5),
    ("rs2", 0, "act", 45.5), ("relu", 2, "act", 45.5), ("up", 3, "pe", 50), ("gated", 1, "dve", 57),
    ("iqT", 0, "act", 60.5), ("absmax", 1, "dve", 63.5), ("scale2", 1, "dve", 67), ("relu", 3, "act", 68.5),
    ("quant2", 1, "dve", 71.5), ("square", 1, "act", 73), ("rs2", 1, "act", 74.5), ("outscale", 1, "dve", 76.5),
    ("final", 0, "dve", 79), ("down", 0, "pe", 80), ("final", 1, "dve", 81.5), ("iqT", 1, "act", 83.5),
    ("iqT", 1, "pe", 84), ("down", 1, "pe", 92.5),
]


def chain(b):
    return FIRST if b == 0 else LAST if b == BATCH - 1 else MIDDLE


FILLS = {
    "setup": [("setup", "act"), ("setup", "act"), ("setup", "dve")], "w": [("w_res", "dve")],
    "ctxT": [("ctxT", "act")], "inproj": [("conv", "dve")], "xdbl": [("split", "dve")], "dtproj": [("absx", "act")],
    "yT": [("x1", "dve")], "xqT": [("xqT", "act")], "up": [("relu", "act"), ("gate", "dve")],
    "iqT": [("iqT", "act"), ("iqT", "act")], "down": [("final", "dve")],
}


def schedule():
    timed = [(t, name, e, 0, i) for name, i, e, t in ONCE]
    for b in range(BATCH):
        timed += [(TICKS * b + t, name, e, b, i) for name, i, e, t in chain(b)]
        timed += [(TICKS * b + GT * g + t, name, e, b, g) for g in range(NG) for name, e, t in CORE]
    timed.sort(key=lambda s: s[0])
    return {e: [(name, b, i) for _, name, en, b, i in timed if en == e] for e in ("pe", "act", "dve", "pool")}


ORDER = schedule()


def number_banks():
    number = {}
    for name, b, i in ORDER["pe"]:
        for n in range(len(FILLS.get(name, []))):
            number[(name, b, i, n)] = len(number)
    by = [None] * len(number)
    for e in ("act", "dve"):
        count = 0
        for step, b, i in ORDER[e]:
            for name, fills in FILLS.items():
                for n, consumer in enumerate(fills):
                    if consumer == (step, e) and (name, b, i, n) in number:
                        count += 1
                        by[number[(name, b, i, n)]] = (e, count)
    return number, by


WORK_AT, WORK_BY = number_banks()


def build(nc, a, out):
    ctx = ExitStack()
    with ctx:
        def sb(name, shape, dt=fp32):
            return ctx.enter_context(nc.sbuf_tensor(name, shape, dt))

        def sem(name):
            return ctx.enter_context(nc.semaphore(name))

        identf = sb("identf", [P, P])
        pick = sb("pick", [P, 2 * NS])
        sel = sb("sel", [P, 2 * NS, P], bf16)
        ctx_in = sb("ctx_in", [P, BATCH * HALVES, DM])
        ctxT = sb("ctxT", [P, 2, L])
        win_in = sb("win_in", [P, HALVES, DM])
        winT = sb("winT", [P, DI])
        xpw_in = sb("xpw_in", [P, DI])
        xpwT = sb("xpwT", [P, HALVES, P])
        dtw_in = sb("dtw_in", [P, HALVES, RANK])
        dtwT = sb("dtwT", [RANK, DI])
        convw = sb("convw", [P, HALVES, TAPS])
        convb = sb("convb", [P, HALVES])
        dtb = sb("dtb", [P, HALVES])
        dskip = sb("dskip", [P, HALVES])
        nega = sb("nega", [P, HALVES, NS])
        gates = sb("gates", [P, 2])
        gtmp = sb("gtmp", [P, 2])
        normw = sb("normw", [P, HID])
        x = sb("x", [P, BATCH, HALVES, L])
        xstat = sb("xstat", [P, BATCH * HALVES, 6])
        xmv = sb("xmv", [P, BATCH * HALVES, 2])
        xrs = sb("xrs", [P, BATCH * HALVES])
        xt1 = sb("xt1", [P, BATCH * HALVES])
        xc = sb("xc", [P, HALVES, L])
        sg = sb("sg", [P, HALVES, L])
        u = sb("u", [P, 2, HALVES, L])
        bcs = sb("bcs", [P, 2, L], bf16)
        bcr = sb("bcr", [P, L])
        dtlow = sb("dtlow", [RANK, 2, L])
        xs = sb("xs", [P, HALVES, L])
        q = sb("q", [P, HALVES, L])
        lw = sb("lw", [P, HALVES, L])
        rr = sb("rr", [P, HALVES, L])
        dt = sb("dt", [P, 2, HALVES, L])
        du = sb("du", [P, 2, HALVES, L])
        lnsmall = sb("lnsmall", [P, 1])
        zn = sb("zn", [P, 2, HALVES, L])
        ze = sb("ze", [P, 2, HALVES, L])
        yd = sb("yd", [P, 2, HALVES, L])
        dA = sb("dA", [P, 2, HALVES, GN, L])
        hb = sb("hb", [P, 3, HALVES, GN * L])
        cs = sb("cs", [P, 2, GN * L])
        edge = sb("edge", [P, HALVES, NS])
        carry = sb("carry", [P, HALVES, NS])
        fstat = sb("fstat", [P, HALVES, 6])
        fmv = sb("fmv", [P, BATCH, HALVES, 2])
        frs = sb("frs", [P, BATCH, HALVES])
        fsd = sb("fsd", [P, BATCH, HALVES])
        gsd = sb("gsd", [P, BATCH, HALVES])
        fam = sb("fam", [P, BATCH, HALVES])
        finv = sb("finv", [P, BATCH, HALVES])
        fs = sb("fs", [P, BATCH, HALVES])
        xn = sb("xn", [P, HALVES, L])
        xqT = sb("xqT", [P, HALVES, HALVES, P], bf16)
        ru = sb("ru", [P, 2, HALVES, HPAD])
        gg = sb("gg", [P, 2, HALVES, HID])
        gw = sb("gw", [P, 2, HALVES, HID])
        ssq = sb("ssq", [P, BATCH, HALVES])
        gv = sb("gv", [P, BATCH, HALVES])
        grs = sb("grs", [P, BATCH, HALVES])
        gt = sb("gt", [P, BATCH, HALVES])
        gam = sb("gam", [P, BATCH, HALVES])
        gc = sb("gc", [P, BATCH, HALVES])
        gos = sb("gos", [P, BATCH, HALVES])
        iqT = sb("iqT", [P, 2, HALVES, FB, P], bf16)
        fin = sb("fin", [P, 2, L])
        w13_in = sb("w13_in", [P, 11, DI])
        w2_in = sb("w2_in", [P, HALVES, HPAD])
        w13T = sb("w13T", [P, 3, HALVES, 2 * HID], bf16)
        w2T = sb("w2T", [P, 3, FB * DI], bf16)
        wres = gg[:, :, :, :].rearrange("p a h f -> p (a h f)")[:, 0:3 * BANK].rearrange("p (n f) -> p n f", n=3)

        b_ps = ctx.enter_context(nc.psum_tensor("b_ps", [P, 2, BANK], fp32))
        c_ps = ctx.enter_context(nc.psum_tensor("c_ps", [P, 2, BANK], fp32))
        y_ps = ctx.enter_context(nc.psum_tensor("y_ps", [P, HALVES, L], fp32))
        w_ps = ctx.enter_context(nc.psum_tensor("w_ps", [P, NWORK, BANK], fp32))

        l_ctx0, l_ctx, l_win, l_small, l_x, l_w13, l_w2, l_nw, l_g = (
            sem(n) for n in ("l_ctx0", "l_ctx", "l_win", "l_small", "l_x", "l_w13", "l_w2", "l_nw", "l_g"))
        pool_k = sem("pool_k")
        act_k = sem("act_k")
        dve_k = sem("dve_k")
        pool_c = sem("pool_c")
        sel_ok = sem("sel_ok")
        work_full = sem("work_full")
        free = {"act": sem("work_free_act"), "dve": sem("work_free_dve")}
        winT_ok, dtwT_ok, nega_ok, gexp_ok = (sem(n) for n in ("winT_ok", "dtwT_ok", "nega_ok", "gexp_ok"))
        gates_ok, xmv_ok, xrs_ok = (sem(n) for n in ("gates_ok", "xmv_ok", "xrs_ok"))
        ctxT_ok, conv_e, clamp_ok, sig_ok, u_ok = (
            sem(n) for n in ("ctxT_ok", "conv_e", "clamp_ok", "sig_ok", "u_ok"))
        dtlow_ok, bcs_ok, abs_ok, q_ok, ql_ok, lw_ok, lns_ok, dt_ok, du_ok = (
            sem(n) for n in ("dtlow_ok", "bcs_ok", "abs_ok", "q_ok", "ql_ok", "lw_ok", "lns_ok", "dt_ok", "du_ok"))
        zn_ok, ze_ok, sz_ok = (sem(n) for n in ("zn_ok", "ze_ok", "sz_ok"))
        b_full, b_free, c_full, cs_ok = (sem(n) for n in ("b_full", "b_free", "c_full", "cs_ok"))
        dA_zero, dA_ok, scan_ok, hc_ok, red_ok = (sem(n) for n in ("dA_zero", "dA_ok", "scan_ok", "hc_ok", "red_ok"))
        edge_x, edge_ok, carry_ok, cut_ok = (sem(n) for n in ("edge_x", "edge_ok", "carry_ok", "cut_ok"))
        yd_ok, yz_ok = (sem(n) for n in ("yd_ok", "yz_ok"))
        fmv_ok, frs_ok, finv_ok, xqm_ok, xqT_ok = (
            sem(n) for n in ("fmv_ok", "frs_ok", "finv_ok", "xqm_ok", "xqT_ok"))
        gg_ok, gw_ok, ssq_ok = (sem(n) for n in ("gg_ok", "gw_ok", "ssq_ok"))
        gv_ok, grs_ok, iq_ok = (
            sem(n) for n in ("gv_ok", "grs_ok", "iq_ok"))
        stored = [sem("stored0"), sem("stored1")]
        whi_ok, wmid_ok, wlo_ok = (sem(n) for n in ("whi_ok", "wmid_ok", "wlo_ok"))

        block = ctx.enter_context(nc.Block())

        def bank(name, b, i, n=0):
            return w_ps[:, WORK_AT[(name, b, i, n)] % NWORK, :]

        def full(name, b, i, n=0):
            return WORK_AT[(name, b, i, n)] + 1

        def emptied(name, b, i, n=0):
            return WORK_BY[WORK_AT[(name, b, i, n)]][1]

        def tokens(b, i):
            return slice(P * tiles(b, i)[0], P * (tiles(b, i)[-1] + 1))

        def summed(b, i):
            return NG // 2 * (i + 1) if b == BATCH - 1 else NG

        def states(buf, b, i):
            return buf.rearrange("p (n l) -> p n l", l=group(b, i)[1])

        def wp_cols(i):
            if i < 6:
                kh, c0 = i // 3, (i % 3) * BANK
                n = min(BANK, 2 * HID - c0)
                return n, [w13T[:, s, kh, c0:c0 + n] for s in range(3)]
            c0 = (i - 6) * BANK
            return BANK, [w2T[:, s, c0:c0 + BANK] for s in range(3)]

        def products(eng, E, name, b, i):
            p = b % 2
            if name == "u":
                eng.wait_ge(sig_ok, b + 1)
                if b >= 2:
                    eng.wait_ge(yd_ok, HALVES * (b - 1))
                E.tensor_tensor(u[:, p], xc[:, :], sg[:, :], ALU.mult).then_inc(u_ok, 1)
            elif name == "du":
                eng.wait_ge(dt_ok, b + 1)
                E.tensor_tensor(du[:, p], dt[:, p], u[:, p], ALU.mult).then_inc(du_ok, 1)
            elif name == "yz":
                eng.wait_ge(sz_ok, b + 1)
                eng.wait_ge(yd_ok, HALVES * (b + i + 1))
                l = tokens(b, i)
                E.tensor_tensor(yd[:, p, :, l], yd[:, p, :, l], ze[:, p, :, l], ALU.mult).then_inc(yz_ok, 1)
            elif name == "gated":
                t = HALVES * b + i
                eng.wait_ge(free["dve"], emptied("up", b, 2 * i + 1, 1))
                E.tensor_tensor(gg[:, p, i], gg[:, p, i], ru[:, p, i, 0:HID], ALU.mult).then_inc(gg_ok, 1)
                eng.wait_ge(gg_ok, t + 1)
                if t == 0:
                    eng.wait_ge(l_nw, 16)
                E.tensor_tensor(gw[:, p, i], gg[:, p, i], normw[:, :], ALU.mult).then_inc(gw_ok, 1)

        @block.sync
        def _(sp):
            ctx_v = a["ctx_1024"].rearrange("b (h p) d -> p (b h) d", p=P)
            x_v = a["x"].rearrange("b (h p) l -> p b h l", p=P)
            xp = a["L0_xattn_x_proj_w"]
            sp.dma_start(ctx_in[:, 0:HALVES, :], ctx_v[:, 0:HALVES, :]).then_inc(l_ctx0, 16)
            sp.dma_start(win_in[:, :, :], a["L0_xattn_in_proj_w"].rearrange("(h p) d -> p h d", p=P)).then_inc(l_win, 16)
            sp.wait_ge(pool_k, 3)
            sp.dma_start(xpw_in[0:RANK, :], xp[0:RANK, :]).then_inc(l_win, 16)
            for r in range(1, 4):
                sp.dma_start(xpw_in[32 * r:32 * r + 2 * NS, :], xp[RANK:RANK + 2 * NS, :]).then_inc(l_win, 16)
            sp.dma_start(dtw_in[:, :, :], a["L0_xattn_dt_proj_w"].rearrange("(h p) r -> p h r", p=P)).then_inc(l_win, 16)
            sp.dma_start(convw[:, :, :], a["L0_xattn_conv_w"].rearrange("(h p) o k -> p h (o k)", p=P)).then_inc(l_small, 16)
            with nc.allow_non_contiguous_dma("one column of channels per half"):
                for t, n in ((convb, "conv_b"), (dtb, "dt_proj_b")):
                    sp.dma_start(t[:, :], a["L0_xattn_" + n].rearrange("(h p) -> p h", p=P)).then_inc(l_small, 16)
            sp.dma_start(nega[:, :, :], a["L0_xattn_A_log"].rearrange("(h p) n -> p h n", p=P)).then_inc(l_small, 16)
            sp.dma_start(w13_in[:, :, :], a["L0_ffn_w13"].rearrange("(t p) d -> p t d", p=P)).then_inc(l_w13, 16)
            sp.dma_start(w2_in[:, :, 0:HID], a["L0_ffn_w2"].rearrange("(h p) f -> p h f", p=P)).then_inc(l_w2, 16)
            sp.dma_start(ctx_in[:, HALVES:, :], ctx_v[:, HALVES:, :]).then_inc(l_ctx, 16)
            sp.dma_start(x[:, :], x_v).then_inc(l_x, 16)
            for i, n in enumerate(("g_xattn", "g_ffn")):
                sp.dma_start(gtmp[:, i:i + 1], a[n].unsqueeze(0).broadcast_to([P, 1])).then_inc(l_g, 16)
            with nc.allow_non_contiguous_dma("one column of channels per half"):
                sp.dma_start(dskip[:, :], a["L0_xattn_D"].rearrange("(h p) -> p h", p=P)).then_inc(l_g, 16)
            sp.dma_start(normw[:, :], a["L0_ffn_norm_w"].unsqueeze(0).broadcast_to([P, HID])).then_inc(l_nw, 16)
            out_v = out.rearrange("b (h p) d -> b h p d", p=P)
            for t in range(BATCH * HALVES):
                sp.wait_ge(free["dve"], emptied("down", t // HALVES, t % HALVES))
                sp.dma_start(out_v[t // HALVES, t % HALVES], fin[:, t % 2, :]).then_inc(stored[t % 2], 16)
            for t in range(2):
                sp.wait_ge(stored[t], 16 * BATCH * HALVES // 2)

        @block.gpsimd
        def _(pool):
            n = [0]

            def link(ins):
                n[0] += 1
                ins.then_inc(pool_c, 1)
                pool.wait_ge(pool_c, n[0])

            nc.gpsimd.memset(identf[:, :], 0.0).then_inc(pool_k, 1)
            nc.gpsimd.memset(pick[:, :], 0.0).then_inc(pool_k, 1)
            nc.gpsimd.memset(xpw_in[:, :], 0.0).then_inc(pool_k, 1)
            nc.gpsimd.memset(lnsmall[:, :], SMALL)
            pool.wait_ge(pool_k, 3)
            nc.gpsimd.affine_select(out=identf[:, :], in_=identf[:, :], compare_op=ALU.not_equal, fill=1.0, base=0,
                                    pattern=[[-1, P]], channel_multiplier=1).then_inc(pool_k, 1)
            for r in range(1, 4):
                link(nc.gpsimd.affine_select(out=pick[:, :], in_=pick[:, :], compare_op=ALU.not_equal, fill=1.0,
                                             base=-32 * r, pattern=[[-1, 2 * NS]], channel_multiplier=1))
            nc.gpsimd.memset(w2_in[:, :, HID:HPAD], 0.0).then_inc(pool_k, 1)
            nc.gpsimd.memset(dA[:, :, :, :, 0:1], 0.0).then_inc(dA_zero, 1)

            for name, b, i in ORDER["pool"]:
                p = b % 2
                k = b * NG + i
                if name in ("u", "du", "yz", "gated"):
                    products(pool, nc.gpsimd, name, b, i)
                elif name == "sz":
                    pool.wait_ge(ze_ok, b + 1)
                    nc.gpsimd.tensor_tensor(ze[:, p], zn[:, p], ze[:, p], ALU.mult).then_inc(sz_ok, 1)
                elif name in ("out0", "out1"):
                    h = int(name[-1])
                    if h == 0:
                        pool.wait_ge(cs_ok, 2 * (k + 1))
                    pool.wait_ge(scan_ok, HALVES * k + h + 1)
                    if b == BATCH - 1 and i < 2:
                        s0, sn = group(b, i)[2:]
                        if i == 0 and h == 0:
                            pool.wait_ge(edge_ok, 1)
                        nc.gpsimd.tensor_tensor(carry[:, h, s0:s0 + sn], states(hb[:, k % 3, h], b, i)[:, :, P - 1],
                                                edge[:, h, s0:s0 + sn], ALU.mult).then_inc(carry_ok, 1)
                        pool.wait_ge(carry_ok, HALVES * i + h + 1)
                    nc.gpsimd.tensor_tensor(hb[:, k % 3, h], hb[:, k % 3, h], cs[:, k % 2], ALU.mult).then_inc(hc_ok, 1)
                elif name == "w_lo":
                    n_, parts = wp_cols(i)
                    pool.wait_ge(wmid_ok, i + 1)
                    nc.gpsimd.tensor_tensor(parts[2], wres[:, i % 3, 0:n_], parts[1], ALU.subtract).then_inc(wlo_ok, 1)

        @block.scalar
        def _(act):
            n = [0]
            act_fn = nc.scalar.activation

            def link(ins):
                n[0] += 1
                ins.then_inc(act_k, 1)
                act.wait_ge(act_k, n[0])

            nc.scalar.preload_act_table_set("natural_log_exp_and_others")
            act.wait_ge(pool_k, 5)

            act_fn(lnsmall[:, :], lnsmall[:, :], ACT.Ln, bias=1.0).then_inc(lns_ok, 1)

            for name, b, i in ORDER["act"]:
                p = b % 2
                k = b * NG + i
                if name == "setup":
                    act.wait_ge(work_full, full("setup", 0, 0, 0))
                    act_fn(winT[:, :], bank("setup", 0, 0, 0)[:, 0:DI], ACT.Copy).then_inc(free["act"], 1)
                    act.wait_ge(work_full, full("setup", 0, 0, 1))
                    act_fn(xpwT[:, :, :].rearrange("p h m -> p (h m)"), bank("setup", 0, 0, 1)[:, 0:DI],
                           ACT.Copy).then_inc(free["act"], 1)
                    act.wait_ge(l_small, 64)
                    link(act_fn(nega[:, :, :], nega[:, :, :], ACT.Exp))
                    act_fn(nega[:, :, :], nega[:, :, :], ACT.Copy, scale=-1.0).then_inc(nega_ok, 1)
                elif name == "sel":
                    act_fn(sel[:, :, :], pick[:, :].unsqueeze(2).broadcast_to([P, 2 * NS, P]), ACT.Copy).then_inc(sel_ok, 1)
                elif name == "ctxT":
                    act.wait_ge(work_full, full("ctxT", b, i))
                    act_fn(ctxT[:, p], bank("ctxT", b, i)[:, 0:L], ACT.Copy).then_inc(free["act"], 1)
                elif name == "sigm0":
                    act.wait_ge(free["dve"], emptied("inproj", b, i))
                    act_fn(sg[:, :], xc[:, :], ACT.Exp, scale=-1.0).then_inc(conv_e, 1)
                elif name == "sigm1":
                    act.wait_ge(clamp_ok, b + 1)
                    link(act_fn(sg[:, :], sg[:, :], ACT.Ln, bias=1.0))
                    act_fn(sg[:, :], sg[:, :], ACT.Exp, scale=-1.0).then_inc(sig_ok, 1)
                elif name == "absx":
                    act.wait_ge(work_full, full("dtproj", b, i))
                    d_ps = bank("dtproj", b, i).rearrange("p (h l) -> p h l", h=HALVES)
                    for h in range(HALVES):
                        last = act_fn(q[:, h], d_ps[:, h], ACT.Abs, bias=dtb[:, h:h + 1])
                    last.then_inc(abs_ok, 1)
                    for h in range(HALVES):
                        last = act_fn(xs[:, h], d_ps[:, h], ACT.Relu, bias=dtb[:, h:h + 1])
                    last.then_inc(free["act"], 1)
                    act.wait_ge(abs_ok, b + 1)
                    act_fn(q[:, :], q[:, :], ACT.Exp, scale=-1.0).then_inc(q_ok, 1)
                elif name == "ln1q":
                    act.wait_ge(ql_ok, b + 1)
                    act_fn(lw[:, :], lw[:, :], ACT.Ln, bias=1.0).then_inc(lw_ok, 1)
                elif name == "xrs":
                    act.wait_ge(xmv_ok, 1)
                    link(act_fn(xrs[:, :], xt1[:, :], ACT.Ln))
                    act_fn(xrs[:, :], xrs[:, :], ACT.Exp, scale=-0.5).then_inc(xrs_ok, 1)
                    act.wait_ge(l_g, 48)
                    act_fn(gates[:, :], gtmp[:, :], ACT.Exp, scale=2.0).then_inc(gexp_ok, 1)
                elif name == "zsig":
                    act.wait_ge(zn_ok, HALVES * (b + 1))
                    if b >= 2:
                        act.wait_ge(yz_ok, b - 1)
                    link(act_fn(ze[:, p], zn[:, p], ACT.Exp, scale=-1.0))
                    link(act_fn(ze[:, p], ze[:, p], ACT.Ln, bias=1.0))
                    act_fn(ze[:, p], ze[:, p], ACT.Exp, scale=-1.0).then_inc(ze_ok, 1)
                elif name in ("decay0", "decay1"):
                    h = int(name[-1])
                    act.wait_ge(dt_ok, b + 1)
                    if k == 0 and h == 0:
                        act.wait_ge(nega_ok, 1)
                    if k >= 2:
                        act.wait_ge(scan_ok, HALVES * (k - 2) + h + 1)
                    l0, ln, s0, sn = group(b, i)
                    dA_g = states(dA[:, k % 2, h].rearrange("p n l -> p (n l)"), b, i)
                    if b == BATCH - 1 and i < 2:
                        act_fn(dA_g[:, :, 0], pick[:, 0:sn], ACT.Copy, scale=0.0).then_inc(cut_ok, 1)
                    for s in range(sn):
                        last = act_fn(dA_g[:, s, 1:ln], dt[:, p, h, l0 + 1:l0 + ln], ACT.Exp,
                                      scale=nega[:, h, s0 + s:s0 + s + 1])
                    last.then_inc(dA_ok, 1)
                elif name == "edge":
                    act.wait_ge(edge_x, HALVES)
                    act_fn(edge[:, :, :], edge[:, :, :], ACT.Exp).then_inc(edge_ok, 1)
                elif name == "c_copy":
                    if k >= 2:
                        act.wait_ge(hc_ok, HALVES * (k - 1))
                    for c in range(2):
                        act.wait_ge(c_full, 2 * k + c + 1)
                        act_fn(cs[:, k % 2, c * BANK:(c + 1) * BANK], c_ps[:, c, :], ACT.Copy).then_inc(cs_ok, 1)
                elif name == "rs1":
                    act.wait_ge(fmv_ok, b + i + 1)
                    ts = slice(tiles(b, i)[0], tiles(b, i)[-1] + 1)
                    link(act_fn(frs[:, b, ts], fs[:, b, ts], ACT.Ln))
                    act_fn(fsd[:, b, ts], frs[:, b, ts], ACT.Exp, scale=0.5)
                    act_fn(frs[:, b, ts], frs[:, b, ts], ACT.Exp, scale=-0.5).then_inc(frs_ok, 1)
                elif name == "xqT":
                    act.wait_ge(work_full, full("xqT", b, i))
                    ts = slice(tiles(b, i)[0], tiles(b, i)[-1] + 1)
                    x_ps = bank("xqT", b, i).rearrange("p (k h t) -> p k h t", k=HALVES, h=HALVES)
                    act_fn(xqT[:, :, ts, :], x_ps[:, :, ts, :], ACT.Copy, bias=-MAGIC).then_inc(free["act"], 1)
                elif name == "relu":
                    h, c = i // 2, i % 2
                    act.wait_ge(work_full, full("up", b, i, 0))
                    act.wait_ge(finv_ok, b + 1 + (h if b == BATCH - 1 else 0))
                    act_fn(ru[:, p, h, c * UC:(c + 1) * UC], bank("up", b, i, 0)[:, 0:UC], ACT.Relu,
                           scale=finv[:, b, h:h + 1]).then_inc(free["act"], 1)
                elif name == "square":
                    act.wait_ge(gw_ok, HALVES * b + i + 1)
                    act_fn(gg[:, p, i], gg[:, p, i], ACT.Square, accum_out=ssq[:, b, i:i + 1]).then_inc(ssq_ok, 1)
                elif name == "rs2":
                    act.wait_ge(gv_ok, b + 1 + i)
                    hs = slice(i, i + 1) if b == BATCH - 1 else slice(0, HALVES)
                    link(act_fn(grs[:, b, hs], gv[:, b, hs], ACT.Ln))
                    act_fn(gsd[:, b, hs], grs[:, b, hs], ACT.Exp, scale=0.5)
                    act_fn(grs[:, b, hs], grs[:, b, hs], ACT.Exp, scale=-0.5).then_inc(grs_ok, 1)
                elif name == "iqT":
                    for c in range(2):
                        act.wait_ge(work_full, full("iqT", b, i, c))
                        act_fn(iqT[:, p, i, 3 * c:3 * c + 3, :].rearrange("p f t -> p (f t)"),
                               bank("iqT", b, i, c)[:, 0:3 * P], ACT.Copy, bias=-MAGIC).then_inc(free["act"], 1)
                elif name == "w_hi":
                    n_, parts = wp_cols(i)
                    act.wait_ge(work_full, full("w", 0, i))
                    act_fn(parts[0], bank("w", 0, i)[:, 0:n_], ACT.Copy).then_inc(whi_ok, 1)
                elif name == "w_mid":
                    n_, parts = wp_cols(i)
                    act.wait_ge(free["dve"], emptied("w", 0, i))
                    act_fn(parts[1], wres[:, i % 3, 0:n_], ACT.Copy).then_inc(wmid_ok, 1)

        @block.vector
        def _(dve):
            V = nc.vector
            n = [0]
            famx, gamx = {}, {}

            def link(ins):
                n[0] += 1
                ins.then_inc(dve_k, 1)
                dve.wait_ge(dve_k, n[0])

            def mark(ins):
                n[0] += 1
                ins.then_inc(dve_k, 1)
                return n[0]

            def newton(y, v, t):
                link(V.tensor_tensor(t, y, y, ALU.mult))
                link(V.tensor_tensor(t, t, v, ALU.mult))
                link(V.tensor_scalar(t, t, -0.5, 1.5, ALU.mult, ALU.add))
                link(V.tensor_tensor(y, y, t, ALU.mult))

            for name, b, i in ORDER["dve"]:
                p = b % 2
                k = b * NG + i
                if name in ("u", "du", "yz", "gated"):
                    products(dve, V, name, b, i)
                elif name == "setup":
                    dve.wait_ge(work_full, full("setup", 0, 0, 2))
                    V.tensor_copy(dtwT[:, :], bank("setup", 0, 0, 2)[0:RANK, 0:DI]).then_inc(free["dve"], 1)
                elif name == "conv":
                    dve.wait_ge(work_full, full("inproj", b, i))
                    if b == 0:
                        dve.wait_ge(l_small, 64)
                    h_ps = bank("inproj", b, i).rearrange("p (h l) -> p h l", h=HALVES)
                    at = [0] * HALVES
                    for h in range(HALVES):
                        at[h] = mark(V.tensor_scalar(xc[:, h], h_ps[:, h], convw[:, h, TAPS - 1:TAPS],
                                                     convb[:, h:h + 1], ALU.mult, ALU.add))
                    for s in range(1, TAPS):
                        for h in range(HALVES):
                            dve.wait_ge(dve_k, at[h])
                            last = V.scalar_tensor_tensor(
                                out=xc[:, h, s:L], in0=h_ps[:, h, 0:L - s], scalar=convw[:, h, TAPS - 1 - s:TAPS - s],
                                in1=xc[:, h, s:L], op0=ALU.mult, op1=ALU.add)
                            if s < TAPS - 1 or h == 0:
                                at[h] = mark(last)
                    last.then_inc(free["dve"], 1)
                elif name == "clamp":
                    dve.wait_ge(conv_e, b + 1)
                    V.tensor_scalar(sg[:, :], sg[:, :], CLAMP, None, ALU.min).then_inc(clamp_ok, 1)
                elif name == "split":
                    x_ps = bank("xdbl", b, i)[:, 0:L]
                    dve.wait_ge(work_full, full("xdbl", b, i))
                    V.tensor_copy(dtlow[:, p], x_ps[0:RANK, :]).then_inc(dtlow_ok, 1)
                    link(V.tensor_copy(bcs[:, p], x_ps))
                    V.tensor_tensor(bcr[:, :], x_ps, bcs[:, p], ALU.subtract).then_inc(free["dve"], 1)
                    dve.wait_ge(free["dve"], emptied("xdbl", b, i))
                    link(V.tensor_copy(bcs[64:P, p], bcr[64:P, :]))
                    V.tensor_tensor(bcs[96:P, p], bcr[96:P, :], bcs[96:P, p], ALU.subtract).then_inc(bcs_ok, 1)
                elif name == "series":
                    dve.wait_ge(q_ok, b + 1)
                    V.tensor_scalar(lw[:, :], q[:, :], SMALL, None, ALU.max).then_inc(ql_ok, 1)
                    dve.wait_ge(ql_ok, b + 1)
                    link(V.tensor_scalar(q[:, :], q[:, :], SMALL, None, ALU.min))
                    link(V.tensor_scalar(rr[:, :], q[:, :], 1.0 / 3.0, -0.5, ALU.mult, ALU.add))
                    link(V.tensor_tensor(rr[:, :], rr[:, :], q[:, :], ALU.mult))
                    link(V.scalar_tensor_tensor(out=q[:, :], in0=rr[:, :], scalar=1.0, in1=q[:, :],
                                                op0=ALU.add, op1=ALU.mult))
                elif name == "dt":
                    dve.wait_ge(lw_ok, b + 1)
                    if b == 0:
                        dve.wait_ge(lns_ok, 1)
                    link(V.scalar_tensor_tensor(out=lw[:, :], in0=lw[:, :], scalar=lnsmall[:, 0:1], in1=q[:, :],
                                                op0=ALU.subtract, op1=ALU.add))
                    dve.wait_ge(free["act"], emptied("dtproj", b, i))
                    V.tensor_tensor(dt[:, p], xs[:, :], lw[:, :], ALU.add).then_inc(dt_ok, 1)
                elif name == "edge":
                    dve.wait_ge(nega_ok, 1)
                    dve.wait_ge(dt_ok, b + 1)
                    for h in range(HALVES):
                        V.tensor_scalar(edge[:, h], nega[:, h], dt[:, p, h, P:P + 1], None, ALU.mult).then_inc(edge_x, 1)
                elif name == "xstat":
                    dve.wait_ge(l_x, 16)
                    for j in range(BATCH * HALVES):
                        at = mark(V.bn_stats(xstat[:, j], x[:, j // HALVES, j % HALVES]))
                    dve.wait_ge(dve_k, at)
                    for j in range(BATCH * HALVES):
                        at = mark(V.bn_aggr(xmv[:, j], xstat[:, j]))
                    dve.wait_ge(dve_k, at)
                    V.tensor_scalar(xt1[:, :], xmv[:, :, 1], EPS, None, ALU.add).then_inc(xmv_ok, 1)
                elif name == "gates":
                    dve.wait_ge(xrs_ok, 1)
                    newton(xrs[:, :], xt1[:, :], xstat[:, :, 0])
                    dve.wait_ge(gexp_ok, 1)
                    link(V.tensor_scalar(gates[:, :], gates[:, :], 1.0, None, ALU.add))
                    link(V.reciprocal(gates[:, :], gates[:, :]))
                    link(V.tensor_scalar(gates[:, :], gates[:, :], -2.0, 1.0, ALU.mult, ALU.add))
                elif name == "z":
                    if b >= 2:
                        dve.wait_ge(sz_ok, b - 1)
                    for h in range(HALVES):
                        j = HALVES * b + h
                        V.tensor_scalar(zn[:, p, h], x[:, b, h], xmv[:, j, 0:1], xrs[:, j:j + 1],
                                        ALU.subtract, ALU.mult).then_inc(zn_ok, 1)
                elif name in ("mix0", "mix1"):
                    h = int(name[-1])
                    if h == 0:
                        dve.wait_ge(du_ok, b + 1)
                        dve.wait_ge(b_full, k + 1)
                    if k >= 3:
                        dve.wait_ge(red_ok, HALVES * (k - 3) + h + 1)
                    l0, ln, s0, sn = group(b, i)
                    V.tensor_tensor(states(hb[:, k % 3, h], b, i), states(b_ps[:, :, :].rearrange("p c m -> p (c m)"), b, i),
                                    du[:, p, h, l0:l0 + ln].unsqueeze(1).broadcast_to([P, sn, ln]),
                                    ALU.mult).then_inc(b_free, 1)
                elif name in ("scan0", "scan1"):
                    h = int(name[-1])
                    if k == 0:
                        dve.wait_ge(dA_zero, 1)
                    dve.wait_ge(dA_ok, HALVES * k + h + 1)
                    dve.wait_ge(b_free, HALVES * k + h + 1)
                    if b == BATCH - 1 and i >= 2:
                        s0, sn = group(b, i)[2:]
                        first_col = states(hb[:, k % 3, h], b, i)[:, :, 0]
                        dve.wait_ge(carry_ok, HALVES * (i - 2) + h + 1)
                        link(V.tensor_tensor(first_col, first_col, carry[:, h, s0:s0 + sn], ALU.add))
                    V.tensor_tensor_scan(hb[:, k % 3, h], dA[:, k % 2, h].rearrange("p n l -> p (n l)"),
                                         hb[:, k % 3, h], 0.0, ALU.mult, ALU.add).then_inc(scan_ok, 1)
                elif name == "yd":
                    dve.wait_ge(red_ok, HALVES * (NG * b + summed(b, i)))
                    l = tokens(b, i)
                    for h in range(HALVES):
                        V.scalar_tensor_tensor(out=yd[:, p, h, l], in0=u[:, p, h, l], scalar=dskip[:, h:h + 1],
                                               in1=y_ps[:, h, l], op0=ALU.mult, op1=ALU.add).then_inc(yd_ok, 1)
                elif name == "x1":
                    dve.wait_ge(work_full, full("yT", b, i))
                    t0, t1 = tiles(b, i)[0], tiles(b, i)[-1] + 1
                    xb = x[:, b, t0:t1].rearrange("p h l -> p (h l)")
                    V.scalar_tensor_tensor(out=xb, in0=bank("yT", b, i)[:, 0:(t1 - t0) * DI], scalar=gates[:, 0:1], in1=xb,
                                           op0=ALU.mult, op1=ALU.add).then_inc(free["dve"], 1)
                    dve.wait_ge(free["dve"], emptied("yT", b, i))
                    for h in range(t0, t1):
                        at = mark(V.bn_stats(fstat[:, h], x[:, b, h]))
                    dve.wait_ge(dve_k, at)
                    for h in range(t0, t1):
                        at = mark(V.bn_aggr(fmv[:, b, h], fstat[:, h]))
                    dve.wait_ge(dve_k, at)
                    V.tensor_scalar(fs[:, b, t0:t1], fmv[:, b, t0:t1, 1], EPS, None, ALU.add).then_inc(fmv_ok, 1)
                    for h in range(t0, t1):
                        at = mark(V.tensor_scalar(xn[:, h], x[:, b, h], fmv[:, b, h, 0:1], None, ALU.subtract))
                    dve.wait_ge(dve_k, at)
                    famx[b, i] = mark(V.tensor_reduce(fam[:, b, t0:t1], xn[:, t0:t1, :], AX.X, ALU.max, apply_absolute_value=True))
                elif name == "quant1":
                    t0, t1 = tiles(b, i)[0], tiles(b, i)[-1] + 1
                    ts = slice(t0, t1)
                    dve.wait_ge(dve_k, famx[b, i])
                    link(V.tensor_scalar(fam[:, b, ts], fam[:, b, ts], 1.0 / 127.0, None, ALU.mult))
                    dve.wait_ge(frs_ok, b + i + 1)
                    link(V.scalar_tensor_tensor(out=fam[:, b, ts], in0=fsd[:, b, ts], scalar=1e-5 / 127.0,
                                                in1=fam[:, b, ts], op0=ALU.mult, op1=ALU.max))
                    link(V.reciprocal(fs[:, b, ts], fam[:, b, ts]))
                    for h in range(t0, t1):
                        V.tensor_scalar(xn[:, h], xn[:, h], fs[:, b, h:h + 1], MAGIC, ALU.mult, ALU.add).then_inc(xqm_ok, 1)
                    V.tensor_tensor(finv[:, b, ts], fam[:, b, ts], frs[:, b, ts], ALU.mult).then_inc(finv_ok, 1)
                elif name == "gate":
                    h, c = i // 2, i % 2
                    dve.wait_ge(work_full, full("up", b, i, 1))
                    dve.wait_ge(free["act"], emptied("up", b, i, 0))
                    V.scalar_tensor_tensor(out=gg[:, p, h, c * UC:(c + 1) * UC], in0=bank("up", b, i, 1)[:, 0:UC],
                                           scalar=finv[:, b, h:h + 1], in1=ru[:, p, h, c * UC:(c + 1) * UC],
                                           op0=ALU.mult, op1=ALU.mult).then_inc(free["dve"], 1)
                elif name == "absmax":
                    dve.wait_ge(gw_ok, HALVES * b + i + 1)
                    at = mark(V.tensor_reduce(gam[:, b, i:i + 1], gw[:, p, i], AX.X, ALU.max, apply_absolute_value=True))
                    if b == BATCH - 1 or i == HALVES - 1:
                        hs = slice(i, i + 1) if b == BATCH - 1 else slice(0, HALVES)
                        dve.wait_ge(ssq_ok, HALVES * b + i + 1)
                        V.tensor_scalar(gv[:, b, hs], ssq[:, b, hs], 1.0 / HID, EPS, ALU.mult, ALU.add).then_inc(gv_ok, 1)
                        dve.wait_ge(dve_k, at)
                        gamx[b, i if b == BATCH - 1 else 0] = mark(V.tensor_scalar(gam[:, b, hs], gam[:, b, hs], 1.0 / 127.0, None, ALU.mult))
                elif name == "scale2":
                    hs = slice(i, i + 1) if b == BATCH - 1 else slice(0, HALVES)
                    dve.wait_ge(grs_ok, b + 1 + i)
                    dve.wait_ge(dve_k, gamx[b, i])
                    link(V.scalar_tensor_tensor(out=gt[:, b, hs], in0=gsd[:, b, hs], scalar=1e-5 / 127.0,
                                                in1=gam[:, b, hs], op0=ALU.mult, op1=ALU.max))
                    link(V.reciprocal(gc[:, b, hs], gt[:, b, hs]))
                    if b == 0:
                        link(V.memset(ru[:, :, :, HID:HPAD], MAGIC))
                elif name == "outscale":
                    hs = slice(i, i + 1) if b == BATCH - 1 else slice(0, HALVES)
                    newton(grs[:, b, hs], gv[:, b, hs], gos[:, b, hs])
                    link(V.scalar_tensor_tensor(out=gos[:, b, hs], in0=gt[:, b, hs], scalar=gates[:, 1:2],
                                                in1=grs[:, b, hs], op0=ALU.mult, op1=ALU.mult))
                elif name == "quant2":
                    V.tensor_scalar(ru[:, p, i, 0:HID], gw[:, p, i], gc[:, b, i:i + 1], MAGIC, ALU.mult, ALU.add).then_inc(iq_ok, 1)
                elif name == "final":
                    t = HALVES * b + i
                    dve.wait_ge(work_full, full("down", b, i))
                    if t >= 2:
                        dve.wait_ge(stored[t % 2], 16 * (t // 2))
                    V.scalar_tensor_tensor(out=fin[:, t % 2], in0=bank("down", b, i)[:, 0:L], scalar=gos[:, b, i:i + 1],
                                           in1=x[:, b, i], op0=ALU.mult, op1=ALU.add).then_inc(free["dve"], 1)
                elif name == "w_res":
                    n_, parts = wp_cols(i)
                    dve.wait_ge(whi_ok, i + 1)
                    if i >= 3:
                        dve.wait_ge(wlo_ok, i - 2)
                    V.tensor_tensor(wres[:, i % 3, 0:n_], bank("w", 0, i)[:, 0:n_], parts[0],
                                    ALU.subtract).then_inc(free["dve"], 1)

        @block.tensor
        def _(pe):
            T = nc.tensor

            def claim(name, b, i, n=0):
                w = WORK_AT[(name, b, i, n)]
                if w >= NWORK:
                    who, count = WORK_BY[w - NWORK]
                    pe.wait_ge(free[who], count)
                return bank(name, b, i, n)

            for name, b, i in ORDER["pe"]:
                p = b % 2
                k = b * NG + i
                if name == "setup":
                    pe.wait_ge(pool_k, 4)
                    pe.wait_ge(l_win, 96)
                    ps = claim("setup", 0, 0, 0)
                    for h in range(HALVES):
                        last = T.transpose(ps[:, h * P:(h + 1) * P], win_in[:, h, :], identf[:, :])
                    last.then_inc(work_full, 1)
                    ps = claim("setup", 0, 0, 1)
                    for h in range(HALVES):
                        last = T.transpose(ps[:, h * P:(h + 1) * P], xpw_in[:, h * P:(h + 1) * P], identf[:, :])
                    last.then_inc(work_full, 1)
                    ps = claim("setup", 0, 0, 2)
                    for h in range(HALVES):
                        last = T.transpose(ps[0:RANK, h * P:(h + 1) * P], dtw_in[:, h, :], identf[:, :])
                    last.then_inc(work_full, 1)
                elif name == "ctxT":
                    pe.wait_ge(l_ctx0 if b == 0 else l_ctx, 16)
                    ps = claim(name, b, i)
                    for h in range(HALVES):
                        last = T.transpose(ps[:, h * P:(h + 1) * P], ctx_in[:, HALVES * b + h, :], identf[:, :])
                    last.then_inc(work_full, 1)
                elif name == "inproj":
                    pe.wait_ge(free["act"], emptied("ctxT", b, i))
                    ps = claim(name, b, i)
                    for h in range(HALVES):
                        last = T.matmul(ps[:, h * L:(h + 1) * L], winT[:, h * P:(h + 1) * P], ctxT[:, p], start=True, stop=True)
                    last.then_inc(work_full, 1)
                elif name == "xdbl":
                    pe.wait_ge(u_ok, b + 1)
                    ps = claim(name, b, i)
                    for h in range(HALVES):
                        last = T.matmul(ps[:, 0:L], xpwT[:, h], u[:, p, h], start=(h == 0), stop=(h == HALVES - 1))
                    last.then_inc(work_full, 1)
                elif name == "dtproj":
                    pe.wait_ge(dtlow_ok, b + 1)
                    if b == 0:
                        pe.wait_ge(free["dve"], emptied("setup", 0, 0, 2))
                    ps = claim(name, b, i)
                    for h in range(HALVES):
                        last = T.matmul(ps[:, h * L:(h + 1) * L], dtwT[:, h * P:(h + 1) * P], dtlow[:, p], start=True, stop=True)
                    last.then_inc(work_full, 1)
                elif name == "bc_b":
                    pe.wait_ge(bcs_ok, b + 1)
                    if k == 0:
                        pe.wait_ge(sel_ok, 1)
                    if k:
                        pe.wait_ge(b_free, HALVES * k)
                    l0, ln, s0, sn = group(b, i)
                    for c in range(2):
                        for s in range(sn // 2):
                            last = T.matmul(b_ps[:, c, s * ln:(s + 1) * ln], sel[:, s0 + sn // 2 * c + s],
                                            bcs[:, p, l0:l0 + ln], start=True, stop=True)
                    last.then_inc(b_full, 1)
                elif name == "bc_c":
                    pe.wait_ge(bcs_ok, b + 1)
                    if k == 0:
                        pe.wait_ge(sel_ok, 1)
                    l0, ln, s0, sn = group(b, i)
                    for c in range(2):
                        if k:
                            pe.wait_ge(cs_ok, 2 * (k - 1) + c + 1)
                        for s in range(sn // 2):
                            last = T.matmul(c_ps[:, c, s * ln:(s + 1) * ln], sel[:, NS + s0 + sn // 2 * c + s],
                                            bcs[:, p, l0:l0 + ln], start=True, stop=True)
                        last.then_inc(c_full, 1)
                elif name in ("sum0", "sum1"):
                    h = int(name[-1])
                    l0, ln, s0, sn = group(b, i)
                    first = s0 == 0 and h == 0
                    if first and k:
                        pe.wait_ge(yd_ok, HALVES * (b + (l0 > 0)))
                    pe.wait_ge(hc_ok, HALVES * k + h + 1)
                    for s in range(sn):
                        last = T.matmul(y_ps[:, h, l0:l0 + ln], identf[:, :], hb[:, k % 3, h, s * ln:(s + 1) * ln],
                                        start=(first and s == 0), stop=(s0 + s == NS - 1), skip_group_check=True)
                    last.then_inc(red_ok, 1)
                elif name == "yT":
                    pe.wait_ge(yz_ok, b + i + 1)
                    ps = claim(name, b, i)
                    for n, t in enumerate(tiles(b, i)):
                        for h in range(HALVES):
                            c = n * DI + h * P
                            last = T.transpose(ps[:, c:c + P], yd[:, p, h, t * P:(t + 1) * P], identf[:, :])
                    last.then_inc(work_full, 1)
                elif name == "xqT":
                    pe.wait_ge(xqm_ok, HALVES * b + tiles(b, i)[-1] + 1)
                    ps = claim(name, b, i)
                    for kh in range(HALVES):
                        for h in tiles(b, i):
                            c = (kh * HALVES + h) * P
                            last = T.transpose(ps[:, c:c + P], xn[:, h, kh * P:(kh + 1) * P], identf[:, :])
                    last.then_inc(work_full, 1)
                elif name == "up":
                    h, c = i // 2, i % 2
                    pe.wait_ge(free["act"], emptied("xqT", b, h if b == BATCH - 1 else 0))
                    if b == 0 and i == 0:
                        pe.wait_ge(wlo_ok, NWP)
                    for j in range(2):
                        ps = claim(name, b, i, j)
                        c0 = j * HID + c * UC
                        for kh in range(HALVES):
                            for s in range(3):
                                last = T.matmul(ps[:, 0:UC], xqT[:, kh, h, :], w13T[:, s, kh, c0:c0 + UC],
                                                start=(kh == 0 and s == 0), stop=(kh == 1 and s == 2))
                        last.then_inc(work_full, 1)
                elif name == "iqT":
                    pe.wait_ge(iq_ok, HALVES * b + i + 1)
                    for c in range(2):
                        ps = claim(name, b, i, c)
                        for f in range(3):
                            last = T.transpose(ps[:, f * P:(f + 1) * P], ru[:, p, i, (3 * c + f) * P:(3 * c + f + 1) * P],
                                               identf[:, :])
                        last.then_inc(work_full, 1)
                elif name == "down":
                    ps = claim(name, b, i)
                    pe.wait_ge(free["act"], emptied("iqT", b, i, 1))
                    for f in range(FB):
                        for s in range(3):
                            last = T.matmul(ps[:, 0:DI], iqT[:, p, i, f, :], w2T[:, s, f * DI:(f + 1) * DI],
                                            start=(f == 0 and s == 0), stop=(f == FB - 1 and s == 2))
                    last.then_inc(work_full, 1)
                elif name == "w":
                    ps = claim(name, b, i)
                    if i < 6:
                        pe.wait_ge(l_w13, 16)
                        kh, t0 = i // 3, (i % 3) * 4
                        for t in range(t0, min(t0 + 4, 11)):
                            last = T.transpose(ps[:, (t - t0) * P:(t - t0 + 1) * P], w13_in[:, t, kh * P:(kh + 1) * P],
                                               identf[:, :])
                    else:
                        pe.wait_ge(l_w2, 16)
                        pe.wait_ge(pool_k, 5)
                        for j in range(4):
                            f, h = 2 * (i - 6) + j // 2, j % 2
                            last = T.transpose(ps[:, j * P:(j + 1) * P], w2_in[:, h, f * P:(f + 1) * P], identf[:, :])
                    last.then_inc(work_full, 1)


def kernel(**inputs):
    import numpy as np
    import concourse.bacc as bacc
    from concourse.bass_utils import run_bass_kernel_spmd

    nc = bacc.Bacc("TRN2", target_bir_lowering=False, num_devices=1)
    arrays, args = {}, {}
    for name, v in inputs.items():
        v = np.ascontiguousarray(v)
        arrays["in_" + name] = v
        args[name] = nc.dram_tensor("in_" + name, v.shape, mybir.dt.from_np(v.dtype), kind="ExternalInput").ap()
    out = nc.dram_tensor("out", (BATCH, L, DI), fp32, kind="ExternalOutput").ap()
    build(nc, args, out)
    r = run_bass_kernel_spmd(nc, [arrays], core_ids=[0])
    return r.results[0]["out"]
```

```python
import concourse.bass as bass
from concourse import mybir
from contextlib import ExitStack

fp32 = mybir.dt.float32
bf16 = mybir.dt.bfloat16
ALU = mybir.AluOpType
ACT = mybir.ActivationFunctionType
AX = mybir.AxisListType

P = 128
BATCH, L, DI = 4, 256, 256
DM = 128
NS, RANK, TAPS = 16, 8, 4
HALVES = DI // P
GN = 4
NG = NS // GN
HID = 704
HPAD = 768
FB = HPAD // P
UC = HID // 2
EPS = 1e-5
MAGIC = 1.5 * 2.0 ** 23
SMALL = 2.0 ** -8
CLAMP = 2.0 ** 60
BANK = 512
NWORK = 3
WARM = (8, 10)
NWP = 9

GT = 4
TICKS = GT * NG
CORE = [
    ("bc_c", "pe", -0.41), ("c_copy", "act", -0.36), ("mix0", "dve", 0.24), ("mix1", "dve", 0.69),
    ("decay0", "act", 0.74), ("bc_b", "pe", 0.79), ("decay1", "act", 1.77), ("scan0", "dve", 1.82),
    ("scan1", "dve", 3.25), ("out0", "pool", 4.57), ("out1", "pool", 4.62), ("sum0", "pe", 7.73),
    ("sum1", "pe", 7.78),
]


def tiles(b, i):
    return range(i, i + 1) if b == BATCH - 1 else range(HALVES)


def group(b, i):
    if b == BATCH - 1:
        return P * (i // 2), P, 2 * GN * (i % 2), 2 * GN
    return 0, L, GN * i, GN


ONCE = [
    ("winT", 0, "pe", -40.7), ("winT", 0, "act", -35.75), ("sel", 0, "act", -33.22), ("xpwT", 0, "act", -23.22),
    ("diag", 0, "pool", -23.17), ("warm", 0, "pe", -22.7), ("dtwT", 0, "dve", -22.58), ("w_hi", 0, "act", -22.45),
    ("w_res", 0, "pool", -19.87), ("nega", 0, "act", -19.27), ("xpwT", 0, "pe", -18.7), ("w_hi", 1, "act", -18.25),
    ("dtwT", 0, "pe", -17.7), ("w", 0, "pe", -16.61), ("w_res", 1, "pool", -15.2), ("w_lo", 0, "pool", -9.2),
    ("w", 1, "pe", -8.2), ("xstat", 0, "dve", -8.15), ("warm", 1, "pe", -6.61), ("w_mid", 0, "act", -6.3),
    ("w_hi", 2, "act", -5.26), ("w_mid", 1, "act", -4.66), ("w", 2, "pe", -3.71), ("xrs", 0, "act", -1.21),
    ("w_hi", 3, "act", 0.65), ("w_mid", 2, "act", 1.7), ("w_res", 2, "pool", 2.25), ("w_hi", 4, "act", 2.45),
    ("w_lo", 1, "pool", 2.5), ("w", 3, "pe", 2.65), ("w_res", 3, "pool", 3.3), ("w_mid", 3, "act", 3.45),
    ("w", 4, "pe", 3.55), ("w_lo", 2, "pool", 4), ("gates", 0, "dve", 5.65), ("w_res", 4, "pool", 5.7),
    ("w", 5, "pe", 6.6), ("w_lo", 3, "pool", 10.1), ("w_hi", 5, "act", 10.5), ("w_mid", 4, "act", 11.75),
    ("w_res", 5, "pool", 12.65), ("w_hi", 6, "act", 17.4), ("w_hi", 7, "act", 18.05), ("w_lo", 4, "pool", 18.45),
    ("w_mid", 5, "act", 18.9), ("w_res", 6, "pool", 19.2), ("w", 6, "pe", 19.6), ("w", 7, "pe", 19.94),
    ("w", 8, "pe", 20.95), ("w_lo", 5, "pool", 23), ("w_hi", 8, "act", 24), ("w_res", 7, "pool", 26.05),
    ("w_mid", 6, "act", 26.6), ("w_mid", 7, "act", 26.85), ("w_lo", 6, "pool", 29.05), ("w_res", 8, "pool", 29.6),
    ("w_lo", 7, "pool", 29.75), ("w_mid", 8, "act", 30), ("w_lo", 8, "pool", 30.8),
]
FIRST = [
    ("conv", 0, "dve", -63.52), ("ctxT", 0, "pe", -50.06), ("ctxT", 0, "act", -47.51), ("tap", 0, "act", -34.56),
    ("inproj", 0, "pe", -27.56), ("sigm0", 0, "act", -25.51), ("sigm1", 0, "act", -25.01),
    ("cubic", 0, "pool", -15.11), ("clamp", 0, "dve", -12.56), ("u", 0, "dve", -10.66), ("xdbl", 0, "pe", -9.21),
    ("split", 0, "dve", -9.11), ("series", 0, "dve", -7.09), ("absx", 0, "act", -6.66), ("dtproj", 0, "pe", -6.64),
    ("du", 0, "pool", -6.61), ("ln1q", 0, "act", -6.14), ("dt", 0, "dve", -4.09), ("dtadd", 0, "dve", -3.64),
    ("skip", 0, "pe", 4.38), ("z", 0, "dve", 6.34), ("zsig", 0, "act", 16.5), ("sz", 0, "pool", 17.95),
    ("yz", 0, "dve", 18.95), ("yT", 0, "pe", 20.9), ("x1", 0, "dve", 22.9), ("rs1", 0, "act", 24.8),
    ("quant1", 0, "dve", 27.26), ("xqT", 0, "act", 29.11), ("xqT", 0, "pe", 29.64), ("relu", 0, "act", 31.19),
    ("relu", 1, "act", 31.73), ("up", 0, "pe", 33.68), ("gate", 0, "dve", 34.23), ("up", 1, "pe", 34.23),
    ("relu", 2, "act", 34.44), ("gate", 1, "dve", 35.27), ("gate", 2, "dve", 36.49), ("up", 2, "pe", 37),
    ("relu", 3, "act", 37.22), ("gated", 0, "pool", 38.47), ("up", 3, "pe", 38.89), ("gate", 3, "dve", 39.42),
    ("square", 0, "act", 39.94), ("gated", 1, "pool", 42.72), ("absmax", 0, "dve", 43.22),
    ("square", 1, "act", 43.89), ("absmax", 1, "dve", 44.18), ("scale2", 0, "dve", 44.27),
    ("quant2", 0, "dve", 44.82), ("rs2", 0, "act", 45.22), ("outscale", 0, "dve", 46.16), ("iqT", 0, "act", 47.11),
    ("quant2", 1, "dve", 48.61), ("iqT", 0, "pe", 48.66), ("iqT", 1, "act", 52.71), ("iqT", 1, "pe", 53.66),
    ("down", 0, "pe", 54.98), ("final", 0, "dve", 55.11), ("down", 1, "pe", 55.38), ("final", 1, "dve", 55.93),
]
MIDDLE = [
    ("ctxT", 0, "act", -35.06), ("ctxT", 0, "pe", -30.01), ("inproj", 0, "pe", -18.75), ("tap", 0, "act", -16.7),
    ("conv", 0, "dve", -16.2), ("clamp", 0, "dve", -14.93), ("sigm0", 0, "act", -14.27), ("sigm1", 0, "act", -10.27),
    ("u", 0, "pool", -8.35), ("split", 0, "dve", -7.39), ("absx", 0, "act", -6.11), ("xdbl", 0, "pe", -5.66),
    ("ln1q", 0, "act", -4.84), ("series", 0, "dve", -4.53), ("dtproj", 0, "pe", -4.3), ("cubic", 0, "dve", -3.53),
    ("dt", 0, "dve", -2.48), ("du", 0, "dve", -0.23), ("dtadd", 0, "pool", 0.09), ("skip", 0, "pe", 5.88),
    ("z", 0, "pool", 10.1), ("zsig", 0, "act", 14.13), ("sz", 0, "pool", 17.26), ("yz", 0, "dve", 20.13),
    ("x1", 0, "dve", 21.05), ("rs1", 0, "act", 22), ("yT", 0, "pe", 22.63), ("quant1", 0, "dve", 25.74),
    ("xqT", 0, "act", 28.12), ("gate", 0, "dve", 28.51), ("relu", 0, "act", 28.96), ("xqT", 0, "pe", 29.13),
    ("up", 0, "pe", 30.79), ("relu", 1, "act", 31.88), ("gate", 1, "dve", 32.58), ("relu", 2, "act", 32.96),
    ("gate", 2, "dve", 32.96), ("relu", 3, "act", 33.51), ("gate", 3, "dve", 33.84), ("gated", 0, "dve", 34.41),
    ("up", 1, "pe", 34.65), ("up", 2, "pe", 34.65), ("up", 3, "pe", 35.7), ("square", 0, "act", 36.15),
    ("gated", 1, "pool", 36.2), ("square", 1, "act", 37.47), ("absmax", 0, "dve", 37.7), ("absmax", 1, "dve", 39.07),
    ("rs2", 0, "act", 40.12), ("scale2", 0, "dve", 40.67), ("quant2", 0, "dve", 40.72), ("iqT", 0, "act", 42.95),
    ("quant2", 1, "dve", 44), ("iqT", 0, "pe", 44.7), ("outscale", 0, "dve", 45.05), ("final", 0, "dve", 45.9),
    ("iqT", 1, "act", 46.85), ("iqT", 1, "pe", 49.69), ("down", 0, "pe", 50.39), ("down", 1, "pe", 54.08),
    ("final", 1, "dve", 56.39),
]
LAST = [
    ("ctxT", 0, "pe", -36.07), ("ctxT", 0, "act", -36.02), ("inproj", 0, "pe", -27), ("tap", 0, "act", -23.32),
    ("conv", 0, "dve", -20.55), ("sigm0", 0, "act", -16.96), ("clamp", 0, "dve", -15.91), ("sigm1", 0, "act", -13.64),
    ("u", 0, "pool", -9.64), ("split", 0, "dve", -8.14), ("xdbl", 0, "pe", -8.13), ("absx", 0, "act", -6.68),
    ("series", 0, "dve", -5.58), ("dtproj", 0, "pe", -5.08), ("ln1q", 0, "act", -4.63), ("dt", 0, "dve", -4.06),
    ("cubic", 0, "pool", -3.45), ("dtadd", 0, "pool", -2.43), ("du", 0, "pool", -2.06), ("edge", 0, "dve", -0.11),
    ("z", 0, "pool", 2.48), ("edge", 0, "act", 3.43), ("zsig", 0, "act", 4.64), ("sz", 0, "pool", 4.77),
    ("skip", 0, "pe", 6.88), ("yz", 0, "dve", 10.82), ("x1", 0, "dve", 12.44), ("skip", 1, "pe", 13.44),
    ("yT", 0, "pe", 13.49), ("rs1", 0, "act", 17.44), ("xqT", 0, "act", 18.94), ("quant1", 0, "dve", 19.89),
    ("yz", 1, "dve", 21.88), ("xqT", 0, "pe", 21.89), ("up", 0, "pe", 23.38), ("relu", 0, "act", 24.93),
    ("gate", 0, "dve", 26.38), ("relu", 1, "act", 26.5), ("gate", 1, "dve", 27.55), ("rs1", 1, "act", 28.1),
    ("up", 1, "pe", 28.55), ("x1", 1, "dve", 28.94), ("yT", 1, "pe", 29.39), ("quant1", 1, "dve", 29.4),
    ("absmax", 0, "dve", 61.97), ("scale2", 0, "dve", 76.47), ("gated", 0, "pool", 80.52), ("xqT", 1, "act", 80.52),
    ("xqT", 1, "pe", 82.57), ("square", 0, "act", 83.02), ("relu", 2, "act", 83.07), ("up", 2, "pe", 99.87),
    ("up", 3, "pe", 100.47), ("gate", 2, "dve", 116.72), ("quant2", 0, "dve", 117.47), ("rs2", 0, "act", 118.87),
    ("iqT", 0, "pe", 123.32), ("gate", 3, "dve", 126.42), ("relu", 3, "act", 134.92), ("iqT", 0, "act", 136.07),
    ("square", 1, "act", 136.37), ("gated", 1, "dve", 139.87), ("rs2", 1, "act", 139.92),
    ("absmax", 1, "dve", 140.87), ("iqT", 1, "act", 151.07), ("down", 0, "pe", 154.17),
    ("outscale", 0, "dve", 156.12), ("scale2", 1, "dve", 159.27), ("quant2", 1, "dve", 159.42),
    ("iqT", 1, "pe", 162.82), ("final", 0, "dve", 165.52), ("down", 1, "pe", 170.47), ("outscale", 1, "dve", 184.02),
    ("final", 1, "dve", 186.65),
]


def chain(b):
    return FIRST if b == 0 else LAST if b == BATCH - 1 else MIDDLE


OUT_END = (BATCH - 1, NG - 1, 1)
PRODUCTS = ("clamp", "z", "u", "cubic", "dtadd", "du", "out0", "out1", "gated")
FILLS = {
    "winT": [("winT", "act")], "xpwT": [("xpwT", "act")], "dtwT": [("dtwT", "dve")], "w": [("w_hi", "act")],
    "ctxT": [("ctxT", "act")], "inproj": [("conv", "dve")], "xdbl": [("split", "dve")], "dtproj": [("absx", "act")],
    "yT": [("x1", "dve")], "xqT": [("xqT", "act")], "up": [("relu", "act"), ("gate", "dve")],
    "iqT": [("iqT", "act"), ("iqT", "act")], "down": [("final", "dve")],
}


def schedule():
    timed = [(t, name, e, 0, i) for name, i, e, t in ONCE]
    for b in range(BATCH):
        for name, i, e, t in chain(b):
            timed.append((TICKS * b + t, name, e, b, i))
        for g in range(NG):
            for name, e, t in CORE:
                if (b, g) == OUT_END[:2] and name == "out1":
                    e = "dve"
                timed.append((TICKS * b + GT * g + t, name, e, b, g))
    timed.sort(key=lambda s: s[0])
    return {e: [(name, b, i) for _, name, en, b, i in timed if en == e] for e in ("pe", "act", "dve", "pool")}


ORDER = schedule()


def number_banks():
    number = {}
    for name, b, i in ORDER["pe"]:
        for n in range(len(FILLS.get(name, []))):
            number[(name, b, i, n)] = len(number)
    by = [None] * len(number)
    for e in ("act", "dve"):
        count = 0
        for step, b, i in ORDER[e]:
            for name, fills in FILLS.items():
                for n, consumer in enumerate(fills):
                    if consumer == (step, e) and (name, b, i, n) in number:
                        count += 1
                        by[number[(name, b, i, n)]] = (e, count)
    return number, by


WORK_AT, WORK_BY = number_banks()


def build(nc, a, out):
    ctx = ExitStack()
    with ctx:
        def sb(name, shape, dt=fp32):
            return ctx.enter_context(nc.sbuf_tensor(name, shape, dt))

        def sem(name):
            return ctx.enter_context(nc.semaphore(name))

        identf = sb("identf", [P, P])
        pick = sb("pick", [P, 2 * NS])
        sel = sb("sel", [P, 2 * NS, P], bf16)
        ctx_in = sb("ctx_in", [P, BATCH * HALVES, DM])
        ctxT = sb("ctxT", [P, 2, L])
        win_in = sb("win_in", [P, HALVES, DM])
        winT = sb("winT", [P, DI])
        xpw_in = sb("xpw_in", [P, DI])
        xpwT = sb("xpwT", [P, HALVES, P])
        dtw_in = sb("dtw_in", [P, HALVES, RANK])
        dtwT = sb("dtwT", [RANK, DI])
        convw = sb("convw", [P, HALVES, TAPS])
        convb = sb("convb", [P, HALVES])
        dtb = sb("dtb", [P, HALVES])
        dskip = sb("dskip", [P, HALVES])
        nega = sb("nega", [P, HALVES, NS])
        gates = sb("gates", [P, 2])
        gtmp = sb("gtmp", [P, 2])
        normw = sb("normw", [P, HID])
        x = sb("x", [P, BATCH, HALVES, L])
        xstat = sb("xstat", [P, BATCH * HALVES, 6])
        xmv = sb("xmv", [P, BATCH * HALVES, 2])
        xrs = sb("xrs", [P, BATCH * HALVES])
        xt1 = sb("xt1", [P, BATCH * HALVES])
        xc = sb("xc", [P, HALVES, L])
        sg = sb("sg", [P, HALVES, L])
        u = sb("u", [P, 2, HALVES, L])
        bcs = sb("bcs", [P, 2, L], bf16)
        bcr = sb("bcr", [P, L])
        dtlow = sb("dtlow", [RANK, 2, L])
        xs = sb("xs", [P, HALVES, L])
        q = sb("q", [P, HALVES, L])
        lw = sb("lw", [P, HALVES, L])
        rr = sb("rr", [P, HALVES, L])
        dt = sb("dt", [P, 2, HALVES, L])
        du = sb("du", [P, 2, HALVES, L])
        shift = sb("shift", [P, 2])
        lnsmall = sb("lnsmall", [P, 1])
        zn = sb("zn", [P, HALVES, L])
        ze = sb("ze", [P, 2, HALVES, L])
        yz = sb("yz", [P, 2, HALVES, L])
        diag = sb("diag", [P, HALVES, P])
        dA = sb("dA", [P, 2, HALVES, GN, L])
        hb = sb("hb", [P, 3, HALVES, GN * L])
        cs = sb("cs", [P, 2, GN * L])
        edge = sb("edge", [P, HALVES, NS])
        carry = sb("carry", [P, HALVES, NS])
        fstat = sb("fstat", [P, HALVES, 6])
        fmv = sb("fmv", [P, BATCH, HALVES, 2])
        frs = sb("frs", [P, BATCH, HALVES])
        fsd = sb("fsd", [P, BATCH, HALVES])
        gsd = sb("gsd", [P, BATCH, HALVES])
        fam = sb("fam", [P, BATCH, HALVES])
        finv = sb("finv", [P, BATCH, HALVES])
        fs = sb("fs", [P, BATCH, HALVES])
        xn = sb("xn", [P, HALVES, L])
        xqT = sb("xqT", [P, HALVES, HALVES, P], bf16)
        ru = sb("ru", [P, 2, HALVES, HPAD])
        gg = sb("gg", [P, 2, HALVES, HID])
        gw = sb("gw", [P, 2, HALVES, HID])
        ssq = sb("ssq", [P, BATCH, HALVES])
        gv = sb("gv", [P, BATCH, HALVES])
        grs = sb("grs", [P, BATCH, HALVES])
        gt = sb("gt", [P, BATCH, HALVES])
        gam = sb("gam", [P, BATCH, HALVES])
        gc = sb("gc", [P, BATCH, HALVES])
        gos = sb("gos", [P, BATCH, HALVES])
        iqT = sb("iqT", [P, 2, HALVES, FB, P], bf16)
        fin = sb("fin", [P, 2, L])
        w13_in = sb("w13_in", [P, 11, DI])
        w2_in = sb("w2_in", [P, HALVES, HPAD])
        w13T = sb("w13T", [P, 3, HALVES, 2 * HID], bf16)
        w2T = sb("w2T", [P, 3, FB * DI], bf16)
        wres = gg[:, :, :, :].rearrange("p a h f -> p (a h f)")[:, 0:3 * BANK].rearrange("p (n f) -> p n f", n=3)

        b_ps = ctx.enter_context(nc.psum_tensor("b_ps", [P, 2, BANK], fp32))
        c_ps = ctx.enter_context(nc.psum_tensor("c_ps", [P, 2, BANK], fp32))
        y_ps = ctx.enter_context(nc.psum_tensor("y_ps", [P, HALVES, L], fp32))
        w_ps = ctx.enter_context(nc.psum_tensor("w_ps", [P, NWORK, BANK], fp32))

        l_ctx0, l_ctx, l_win, l_conv, l_xpw, l_dtw, l_dtb, l_alog, l_x, l_w13, l_w2, l_nw, l_g, l_d = (
            sem(n) for n in ("l_ctx0", "l_ctx", "l_win", "l_conv", "l_xpw", "l_dtw", "l_dtb", "l_alog", "l_x",
                             "l_w13", "l_w2", "l_nw", "l_g", "l_d"))
        pool_k = sem("pool_k")
        act_k = sem("act_k")
        dve_k = sem("dve_k")
        pool_c = sem("pool_c")
        sel_ok = sem("sel_ok")
        work_full = sem("work_full")
        free = {e: sem("work_free_" + e) for e in ("act", "dve")}
        nega_ok, gexp_ok = (sem(n) for n in ("nega_ok", "gexp_ok"))
        gates_ok, xmv_ok, xrs_ok = (sem(n) for n in ("gates_ok", "xmv_ok", "xrs_ok"))
        conv_e, clamp_ok, sig_ok, u_ok = (sem(n) for n in ("conv_e", "clamp_ok", "sig_ok", "u_ok"))
        dtlow_ok, bcs_ok, abs_ok, q_ok, lw_ok, ln_ok, lns_ok, dt_ok, du_ok = (
            sem(n) for n in ("dtlow_ok", "bcs_ok", "abs_ok", "q_ok", "lw_ok", "ln_ok", "lns_ok", "dt_ok", "du_ok"))
        tap_ok = sem("tap_ok")
        rr_ok, cubic_ok, soft_ok = (sem(n) for n in ("rr_ok", "cubic_ok", "soft_ok"))
        zn_ok, ze_ok, sz_ok = (sem(n) for n in ("zn_ok", "ze_ok", "sz_ok"))
        b_full, b_free, c_full, cs_ok = (sem(n) for n in ("b_full", "b_free", "c_full", "cs_ok"))
        dA_zero, dA_ok, scan_ok, red_ok = (sem(n) for n in ("dA_zero", "dA_ok", "scan_ok", "red_ok"))
        hc_ok = [sem("hc_ok0"), sem("hc_ok1")]
        hc_end = sem("hc_end")
        edge_x, edge_ok, carry_ok, cut_ok = (sem(n) for n in ("edge_x", "edge_ok", "carry_ok", "cut_ok"))
        diag_ok, yz_ok = (sem(n) for n in ("diag_ok", "yz_ok"))
        fmv_ok, frs_ok, finv_ok, xqm_ok = (sem(n) for n in ("fmv_ok", "frs_ok", "finv_ok", "xqm_ok"))
        gg_ok, gw_ok, ssq_ok = ([sem(n + str(t)) for t in range(HALVES)] for n in ("gg_ok", "gw_ok", "ssq_ok"))
        gv_ok, grs_ok, iq_ok = (
            sem(n) for n in ("gv_ok", "grs_ok", "iq_ok"))
        stored = [sem("stored0"), sem("stored1")]
        wres_ok, wmid_ok, wlo_ok = (sem(n) for n in ("wres_ok", "wmid_ok", "wlo_ok"))

        block = ctx.enter_context(nc.Block())

        def bank(name, b, i, n=0):
            return w_ps[:, WORK_AT[(name, b, i, n)] % NWORK, :]

        def full(name, b, i, n=0):
            return WORK_AT[(name, b, i, n)] + 1

        def emptied(name, b, i, n=0):
            return WORK_BY[WORK_AT[(name, b, i, n)]][1]

        def tokens(b, i):
            return slice(P * tiles(b, i)[0], P * (tiles(b, i)[-1] + 1))

        def summed(b, i):
            return NG // 2 * (i + 1) if b == BATCH - 1 else NG

        def states(buf, b, i):
            return buf.rearrange("p (n l) -> p n l", l=group(b, i)[1])

        def wp_cols(i):
            if i < 6:
                kh, c0 = i // 3, (i % 3) * BANK
                n = min(BANK, 2 * HID - c0)
                return n, [w13T[:, s, kh, c0:c0 + n] for s in range(3)]
            c0 = (i - 6) * BANK
            return BANK, [w2T[:, s, c0:c0 + BANK] for s in range(3)]

        def products(eng, E, name, b, i):
            p = b % 2
            if name == "u":
                eng.wait_ge(sig_ok, b + 1)
                if b >= 2:
                    eng.wait_ge(yz_ok, b - 1)
                E.tensor_tensor(u[:, p], xc[:, :], sg[:, :], ALU.mult).then_inc(u_ok, 1)
            elif name == "clamp":
                eng.wait_ge(conv_e, b + 1)
                E.tensor_scalar(sg[:, :], sg[:, :], CLAMP, None, ALU.min).then_inc(clamp_ok, 1)
            elif name == "z":
                eng.wait_ge(gates_ok, 1)
                if b >= 1:
                    eng.wait_ge(sz_ok, b)
                for h in range(HALVES):
                    j = HALVES * b + h
                    E.tensor_scalar(zn[:, h], x[:, b, h], xmv[:, j, 0:1], xrs[:, j:j + 1],
                                    ALU.subtract, ALU.mult).then_inc(zn_ok, 1)
            elif name in ("out0", "out1"):
                k, h = b * NG + i, int(name[-1])
                eng.wait_ge(cs_ok, 2 * (k + 1))
                eng.wait_ge(scan_ok, HALVES * k + h + 1)
                if b == BATCH - 1 and i < 2:
                    s0, sn = group(b, i)[2:]
                    eng.wait_ge(edge_ok, 1)
                    E.tensor_tensor(carry[:, h, s0:s0 + sn], states(hb[:, k % 3, h], b, i)[:, :, P - 1],
                                    edge[:, h, s0:s0 + sn], ALU.mult).then_inc(carry_ok, 1)
                    eng.wait_ge(carry_ok, HALVES * i + h + 1)
                E.tensor_tensor(hb[:, k % 3, h], hb[:, k % 3, h], cs[:, k % 2],
                                ALU.mult).then_inc(hc_end if (b, i, h) == OUT_END else hc_ok[h], 1)
            elif name == "cubic":
                eng.wait_ge(rr_ok, b + 1)
                E.tensor_tensor(rr[:, :], rr[:, :], q[:, :], ALU.mult).then_inc(cubic_ok, 1)
            elif name == "dtadd":
                eng.wait_ge(soft_ok, b + 1)
                eng.wait_ge(free["act"], emptied("dtproj", b, i))
                E.tensor_tensor(dt[:, p], xs[:, :], lw[:, :], ALU.add).then_inc(dt_ok, 1)
            elif name == "du":
                eng.wait_ge(dt_ok, b + 1)
                E.tensor_tensor(du[:, p], dt[:, p], u[:, p], ALU.mult).then_inc(du_ok, 1)
            elif name == "gated":
                eng.wait_ge(free["dve"], emptied("up", b, 2 * i + 1, 1))
                E.tensor_tensor(gg[:, p, i], gg[:, p, i], ru[:, p, i, 0:HID], ALU.mult).then_inc(gg_ok[i], 1)
                eng.wait_ge(gg_ok[i], b + 1)
                eng.wait_ge(l_nw, 16)
                E.tensor_tensor(gw[:, p, i], gg[:, p, i], normw[:, :], ALU.mult).then_inc(gw_ok[i], 1)

        @block.sync
        def _(sp):
            ctx_v = a["ctx_1024"].rearrange("b (h p) d -> p (b h) d", p=P)
            x_v = a["x"].rearrange("b (h p) l -> p b h l", p=P)
            xp = a["L0_xattn_x_proj_w"]
            def small(t, n):
                with nc.allow_non_contiguous_dma("one column of channels per half"):
                    return sp.dma_start(t[:, :], a["L0_xattn_" + n].rearrange("(h p) -> p h", p=P))

            sp.dma_start(ctx_in[:, 0:HALVES, :], ctx_v[:, 0:HALVES, :]).then_inc(l_ctx0, 16)
            sp.dma_start(win_in[:, :, :], a["L0_xattn_in_proj_w"].rearrange("(h p) d -> p h d", p=P)).then_inc(l_win, 16)
            sp.dma_start(convw[:, :, :], a["L0_xattn_conv_w"].rearrange("(h p) o k -> p h (o k)", p=P)).then_inc(l_conv, 16)
            small(convb, "conv_b").then_inc(l_conv, 16)
            sp.wait_ge(pool_k, 3)
            sp.dma_start(xpw_in[0:RANK, :], xp[0:RANK, :]).then_inc(l_xpw, 16)
            for r in range(1, 4):
                sp.dma_start(xpw_in[32 * r:32 * r + 2 * NS, :], xp[RANK:RANK + 2 * NS, :]).then_inc(l_xpw, 16)
            sp.dma_start(dtw_in[:, :, :], a["L0_xattn_dt_proj_w"].rearrange("(h p) r -> p h r", p=P)).then_inc(l_dtw, 16)
            small(dtb, "dt_proj_b").then_inc(l_dtb, 16)
            sp.dma_start(nega[:, :, :], a["L0_xattn_A_log"].rearrange("(h p) n -> p h n", p=P)).then_inc(l_alog, 16)
            sp.dma_start(w13_in[:, :, :], a["L0_ffn_w13"].rearrange("(t p) d -> p t d", p=P)).then_inc(l_w13, 16)
            sp.dma_start(w2_in[:, :, 0:HID], a["L0_ffn_w2"].rearrange("(h p) f -> p h f", p=P)).then_inc(l_w2, 16)
            sp.dma_start(ctx_in[:, HALVES:, :], ctx_v[:, HALVES:, :]).then_inc(l_ctx, 16)
            sp.dma_start(x[:, :], x_v).then_inc(l_x, 16)
            for i, n in enumerate(("g_xattn", "g_ffn")):
                sp.dma_start(gtmp[:, i:i + 1], a[n].unsqueeze(0).broadcast_to([P, 1])).then_inc(l_g, 16)
            small(dskip, "D").then_inc(l_d, 16)
            sp.dma_start(normw[:, :], a["L0_ffn_norm_w"].unsqueeze(0).broadcast_to([P, HID])).then_inc(l_nw, 16)
            out_v = out.rearrange("b (h p) d -> b h p d", p=P)
            for t in range(BATCH * HALVES):
                sp.wait_ge(free["dve"], emptied("down", t // HALVES, t % HALVES))
                sp.dma_start(out_v[t // HALVES, t % HALVES], fin[:, t % 2, :]).then_inc(stored[t % 2], 16)
            for t in range(2):
                sp.wait_ge(stored[t], 16 * BATCH * HALVES // 2)

        @block.gpsimd
        def _(pool):
            n = [0]

            def link(ins):
                n[0] += 1
                ins.then_inc(pool_c, 1)
                pool.wait_ge(pool_c, n[0])

            nc.gpsimd.memset(identf[:, :], 0.0).then_inc(pool_k, 1)
            nc.gpsimd.memset(pick[:, :], 0.0).then_inc(pool_k, 1)
            nc.gpsimd.memset(xpw_in[:, :], 0.0).then_inc(pool_k, 1)
            nc.gpsimd.memset(lnsmall[:, :], SMALL)
            nc.gpsimd.memset(shift[:, 0:1], -SMALL)
            nc.gpsimd.memset(shift[:, 1:2], 1.0 + SMALL)
            pool.wait_ge(pool_k, 3)
            nc.gpsimd.affine_select(out=identf[:, :], in_=identf[:, :], compare_op=ALU.not_equal, fill=1.0, base=0,
                                    pattern=[[-1, P]], channel_multiplier=1).then_inc(pool_k, 1)
            for r in range(1, 4):
                link(nc.gpsimd.affine_select(out=pick[:, :], in_=pick[:, :], compare_op=ALU.not_equal, fill=1.0,
                                             base=-32 * r, pattern=[[-1, 2 * NS]], channel_multiplier=1))
            nc.gpsimd.memset(w2_in[:, :, HID:HPAD], 0.0).then_inc(pool_k, 1)
            nc.gpsimd.memset(dA[:, :, :, :, 0:1], 0.0).then_inc(dA_zero, 1)

            for name, b, i in ORDER["pool"]:
                p = b % 2
                k = b * NG + i
                if name in PRODUCTS:
                    products(pool, nc.gpsimd, name, b, i)
                elif name == "sz":
                    pool.wait_ge(ze_ok, b + 1)
                    nc.gpsimd.tensor_tensor(ze[:, p], zn[:, :], ze[:, p], ALU.mult).then_inc(sz_ok, 1)
                elif name == "diag":
                    pool.wait_ge(l_d, 16)
                    for h in range(HALVES):
                        nc.gpsimd.tensor_scalar(diag[:, h], identf[:, :], dskip[:, h:h + 1], None,
                                                ALU.mult).then_inc(diag_ok, 1)
                elif name == "w_res":
                    n_, parts = wp_cols(i)
                    pool.wait_ge(free["act"], emptied("w", 0, i))
                    nc.gpsimd.tensor_tensor(wres[:, i % 3, 0:n_], wres[:, i % 3, 0:n_], parts[0],
                                            ALU.subtract).then_inc(wres_ok, 1)
                elif name == "w_lo":
                    n_, parts = wp_cols(i)
                    pool.wait_ge(wmid_ok, i + 1)
                    nc.gpsimd.tensor_tensor(parts[2], wres[:, i % 3, 0:n_], parts[1], ALU.subtract).then_inc(wlo_ok, 1)

        @block.scalar
        def _(act):
            n = [0]
            act_fn = nc.scalar.activation

            def link(ins):
                n[0] += 1
                ins.then_inc(act_k, 1)
                act.wait_ge(act_k, n[0])

            nc.scalar.preload_act_table_set("natural_log_exp_and_others")
            act.wait_ge(pool_k, 5)

            act_fn(lnsmall[:, :], lnsmall[:, :], ACT.Ln, bias=1.0).then_inc(lns_ok, 1)

            for name, b, i in ORDER["act"]:
                p = b % 2
                k = b * NG + i
                if name == "winT":
                    act.wait_ge(work_full, full("winT", 0, 0))
                    act_fn(winT[:, :], bank("winT", 0, 0)[:, 0:DI], ACT.Copy).then_inc(free["act"], 1)
                elif name == "xpwT":
                    act.wait_ge(work_full, full("xpwT", 0, 0))
                    act_fn(xpwT[:, :, :].rearrange("p h m -> p (h m)"), bank("xpwT", 0, 0)[:, 0:DI],
                           ACT.Copy).then_inc(free["act"], 1)
                elif name == "nega":
                    act.wait_ge(l_alog, 16)
                    link(act_fn(nega[:, :, :], nega[:, :, :], ACT.Exp))
                    act_fn(nega[:, :, :], nega[:, :, :], ACT.Copy, scale=-1.0).then_inc(nega_ok, 1)
                elif name == "sel":
                    act_fn(sel[:, :, :], pick[:, :].unsqueeze(2).broadcast_to([P, 2 * NS, P]), ACT.Copy).then_inc(sel_ok, 1)
                elif name == "ctxT":
                    act.wait_ge(work_full, full("ctxT", b, i))
                    act_fn(ctxT[:, p], bank("ctxT", b, i)[:, 0:L], ACT.Copy).then_inc(free["act"], 1)
                elif name == "tap":
                    act.wait_ge(work_full, full("inproj", b, i))
                    if b == 0:
                        act.wait_ge(l_conv, 32)
                    if b:
                        act.wait_ge(u_ok, b)
                    for h in range(HALVES):
                        act_fn(xc[:, h], bank("inproj", b, i)[:, h * L:(h + 1) * L], ACT.Identity,
                               scale=convw[:, h, TAPS - 1:TAPS], bias=convb[:, h:h + 1]).then_inc(tap_ok, 1)
                elif name == "sigm0":
                    act.wait_ge(free["dve"], emptied("inproj", b, i))
                    act_fn(sg[:, :], xc[:, :], ACT.Exp, scale=-1.0).then_inc(conv_e, 1)
                elif name == "sigm1":
                    act.wait_ge(clamp_ok, b + 1)
                    link(act_fn(sg[:, :], sg[:, :], ACT.Ln, bias=1.0))
                    act_fn(sg[:, :], sg[:, :], ACT.Exp, scale=-1.0).then_inc(sig_ok, 1)
                elif name == "absx":
                    act.wait_ge(work_full, full("dtproj", b, i))
                    if b == 0:
                        act.wait_ge(l_dtb, 16)
                    else:
                        act.wait_ge(dt_ok, b)
                    d_ps = bank("dtproj", b, i).rearrange("p (h l) -> p h l", h=HALVES)
                    for h in range(HALVES):
                        last = act_fn(q[:, h], d_ps[:, h], ACT.Abs, bias=dtb[:, h:h + 1])
                    last.then_inc(abs_ok, 1)
                    for h in range(HALVES):
                        last = act_fn(xs[:, h], d_ps[:, h], ACT.Relu, bias=dtb[:, h:h + 1])
                    last.then_inc(free["act"], 1)
                    act.wait_ge(abs_ok, b + 1)
                    act_fn(q[:, :], q[:, :], ACT.Exp, scale=-1.0).then_inc(q_ok, 1)
                elif name == "ln1q":
                    act.wait_ge(q_ok, b + 1)
                    if b:
                        act.wait_ge(soft_ok, b)
                    act_fn(lw[:, :], q[:, :], ACT.Relu, bias=shift[:, 0:1]).then_inc(lw_ok, 1)
                    act.wait_ge(lw_ok, b + 1)
                    act_fn(lw[:, :], lw[:, :], ACT.Ln, bias=shift[:, 1:2]).then_inc(ln_ok, 1)
                elif name == "xrs":
                    act.wait_ge(xmv_ok, 1)
                    link(act_fn(xrs[:, :], xt1[:, :], ACT.Ln))
                    act_fn(xrs[:, :], xrs[:, :], ACT.Exp, scale=-0.5).then_inc(xrs_ok, 1)
                    act.wait_ge(l_g, 32)
                    act_fn(gates[:, :], gtmp[:, :], ACT.Exp, scale=2.0).then_inc(gexp_ok, 1)
                elif name == "zsig":
                    act.wait_ge(zn_ok, HALVES * (b + 1))
                    if b >= 2:
                        act.wait_ge(yz_ok, b - 1)
                    link(act_fn(ze[:, p], zn[:, :], ACT.Exp, scale=-1.0))
                    link(act_fn(ze[:, p], ze[:, p], ACT.Ln, bias=1.0))
                    act_fn(ze[:, p], ze[:, p], ACT.Exp, scale=-1.0).then_inc(ze_ok, 1)
                elif name in ("decay0", "decay1"):
                    h = int(name[-1])
                    act.wait_ge(dt_ok, b + 1)
                    if k == 0 and h == 0:
                        act.wait_ge(nega_ok, 1)
                    if k >= 2:
                        act.wait_ge(scan_ok, HALVES * (k - 2) + h + 1)
                    l0, ln, s0, sn = group(b, i)
                    dA_g = states(dA[:, k % 2, h].rearrange("p n l -> p (n l)"), b, i)
                    if b == BATCH - 1 and i < 2:
                        act_fn(dA_g[:, :, 0], pick[:, 0:sn], ACT.Copy, scale=0.0).then_inc(cut_ok, 1)
                    for s in range(sn):
                        last = act_fn(dA_g[:, s, 1:ln], dt[:, p, h, l0 + 1:l0 + ln], ACT.Exp,
                                      scale=nega[:, h, s0 + s:s0 + s + 1])
                    last.then_inc(dA_ok, 1)
                elif name == "edge":
                    act.wait_ge(edge_x, HALVES)
                    act_fn(edge[:, :, :], edge[:, :, :], ACT.Exp).then_inc(edge_ok, 1)
                elif name == "c_copy":
                    if k >= 2:
                        for h in range(HALVES):
                            act.wait_ge(hc_ok[h], k - 1)
                    for c in range(2):
                        act.wait_ge(c_full, 2 * k + c + 1)
                        act_fn(cs[:, k % 2, c * BANK:(c + 1) * BANK], c_ps[:, c, :], ACT.Copy).then_inc(cs_ok, 1)
                elif name == "rs1":
                    act.wait_ge(fmv_ok, b + i + 1)
                    ts = slice(tiles(b, i)[0], tiles(b, i)[-1] + 1)
                    link(act_fn(frs[:, b, ts], fs[:, b, ts], ACT.Ln))
                    act_fn(fsd[:, b, ts], frs[:, b, ts], ACT.Exp, scale=0.5)
                    act_fn(frs[:, b, ts], frs[:, b, ts], ACT.Exp, scale=-0.5).then_inc(frs_ok, 1)
                elif name == "xqT":
                    act.wait_ge(work_full, full("xqT", b, i))
                    ts = slice(tiles(b, i)[0], tiles(b, i)[-1] + 1)
                    x_ps = bank("xqT", b, i).rearrange("p (k h t) -> p k h t", k=HALVES, h=HALVES)
                    act_fn(xqT[:, :, ts, :], x_ps[:, :, ts, :], ACT.Copy, bias=-MAGIC).then_inc(free["act"], 1)
                elif name == "relu":
                    h, c = i // 2, i % 2
                    act.wait_ge(work_full, full("up", b, i, 0))
                    act.wait_ge(finv_ok, b + 1 + (h if b == BATCH - 1 else 0))
                    act_fn(ru[:, p, h, c * UC:(c + 1) * UC], bank("up", b, i, 0)[:, 0:UC], ACT.Relu,
                           scale=finv[:, b, h:h + 1]).then_inc(free["act"], 1)
                elif name == "square":
                    act.wait_ge(gg_ok[i], b + 1)
                    act_fn(ru[:, p, i, 0:HID], gg[:, p, i], ACT.Square,
                           accum_out=ssq[:, b, i:i + 1]).then_inc(ssq_ok[i], 1)
                elif name == "rs2":
                    act.wait_ge(gv_ok, b + 1 + i)
                    hs = slice(i, i + 1) if b == BATCH - 1 else slice(0, HALVES)
                    link(act_fn(grs[:, b, hs], gv[:, b, hs], ACT.Ln))
                    act_fn(gsd[:, b, hs], grs[:, b, hs], ACT.Exp, scale=0.5)
                    act_fn(grs[:, b, hs], grs[:, b, hs], ACT.Exp, scale=-0.5).then_inc(grs_ok, 1)
                elif name == "iqT":
                    for c in range(2):
                        act.wait_ge(work_full, full("iqT", b, i, c))
                        act_fn(iqT[:, p, i, 3 * c:3 * c + 3, :].rearrange("p f t -> p (f t)"),
                               bank("iqT", b, i, c)[:, 0:3 * P], ACT.Copy, bias=-MAGIC).then_inc(free["act"], 1)
                elif name == "w_hi":
                    n_, parts = wp_cols(i)
                    act.wait_ge(work_full, full("w", 0, i))
                    act_fn(parts[0], bank("w", 0, i)[:, 0:n_], ACT.Copy)
                    if i >= 3:
                        act.wait_ge(wlo_ok, i - 2)
                    act_fn(wres[:, i % 3, 0:n_], bank("w", 0, i)[:, 0:n_], ACT.Copy).then_inc(free["act"], 1)
                elif name == "w_mid":
                    n_, parts = wp_cols(i)
                    act.wait_ge(wres_ok, i + 1)
                    act_fn(parts[1], wres[:, i % 3, 0:n_], ACT.Copy).then_inc(wmid_ok, 1)

        @block.vector
        def _(dve):
            V = nc.vector
            n = [0]
            famx, gamx = {}, {}

            def link(ins):
                n[0] += 1
                ins.then_inc(dve_k, 1)
                dve.wait_ge(dve_k, n[0])

            def mark(ins):
                n[0] += 1
                ins.then_inc(dve_k, 1)
                return n[0]

            def newton(y, v, t):
                link(V.tensor_tensor(t, y, y, ALU.mult))
                link(V.tensor_tensor(t, t, v, ALU.mult))
                link(V.tensor_scalar(t, t, -0.5, 1.5, ALU.mult, ALU.add))
                link(V.tensor_tensor(y, y, t, ALU.mult))

            for name, b, i in ORDER["dve"]:
                p = b % 2
                k = b * NG + i
                if name in PRODUCTS:
                    products(dve, V, name, b, i)
                elif name == "dtwT":
                    dve.wait_ge(work_full, full("dtwT", 0, 0))
                    V.tensor_copy(dtwT[:, :], bank("dtwT", 0, 0)[0:RANK, 0:DI]).then_inc(free["dve"], 1)
                elif name == "conv":
                    h_ps = bank("inproj", b, i).rearrange("p (h l) -> p h l", h=HALVES)
                    dve.wait_ge(tap_ok, HALVES * (b + 1))
                    at = [0] * HALVES
                    for s in range(1, TAPS):
                        for h in range(HALVES):
                            if s > 1:
                                dve.wait_ge(dve_k, at[h])
                            last = V.scalar_tensor_tensor(
                                out=xc[:, h, s:L], in0=h_ps[:, h, 0:L - s], scalar=convw[:, h, TAPS - 1 - s:TAPS - s],
                                in1=xc[:, h, s:L], op0=ALU.mult, op1=ALU.add)
                            if s < TAPS - 1 or h == 0:
                                at[h] = mark(last)
                    last.then_inc(free["dve"], 1)
                elif name == "split":
                    x_ps = bank("xdbl", b, i)[:, 0:L]
                    dve.wait_ge(work_full, full("xdbl", b, i))
                    V.tensor_copy(dtlow[:, p], x_ps[0:RANK, :]).then_inc(dtlow_ok, 1)
                    link(V.tensor_copy(bcs[:, p], x_ps))
                    V.tensor_tensor(bcr[:, :], x_ps, bcs[:, p], ALU.subtract).then_inc(free["dve"], 1)
                    dve.wait_ge(free["dve"], emptied("xdbl", b, i))
                    link(V.tensor_copy(bcs[64:P, p], bcr[64:P, :]))
                    V.tensor_tensor(bcs[96:P, p], bcr[96:P, :], bcs[96:P, p], ALU.subtract).then_inc(bcs_ok, 1)
                elif name == "series":
                    dve.wait_ge(q_ok, b + 1)
                    dve.wait_ge(lw_ok, b + 1)
                    link(V.tensor_scalar(q[:, :], q[:, :], SMALL, None, ALU.min))
                    V.tensor_scalar(rr[:, :], q[:, :], 1.0 / 3.0, -0.5, ALU.mult, ALU.add).then_inc(rr_ok, 1)
                elif name == "dt":
                    dve.wait_ge(ln_ok, b + 1)
                    if b == 0:
                        dve.wait_ge(lns_ok, 1)
                    dve.wait_ge(cubic_ok, b + 1)
                    link(V.scalar_tensor_tensor(out=q[:, :], in0=rr[:, :], scalar=1.0, in1=q[:, :],
                                                op0=ALU.add, op1=ALU.mult))
                    V.scalar_tensor_tensor(out=lw[:, :], in0=lw[:, :], scalar=lnsmall[:, 0:1], in1=q[:, :],
                                           op0=ALU.subtract, op1=ALU.add).then_inc(soft_ok, 1)
                elif name == "edge":
                    dve.wait_ge(nega_ok, 1)
                    dve.wait_ge(dt_ok, b + 1)
                    for h in range(HALVES):
                        V.tensor_scalar(edge[:, h], nega[:, h], dt[:, p, h, P:P + 1], None, ALU.mult).then_inc(edge_x, 1)
                elif name == "xstat":
                    dve.wait_ge(l_x, 16)
                    for j in range(BATCH * HALVES):
                        at = mark(V.bn_stats(xstat[:, j], x[:, j // HALVES, j % HALVES]))
                    dve.wait_ge(dve_k, at)
                    for j in range(BATCH * HALVES):
                        at = mark(V.bn_aggr(xmv[:, j], xstat[:, j]))
                    dve.wait_ge(dve_k, at)
                    V.tensor_scalar(xt1[:, :], xmv[:, :, 1], EPS, None, ALU.add).then_inc(xmv_ok, 1)
                elif name == "gates":
                    dve.wait_ge(xrs_ok, 1)
                    newton(xrs[:, :], xt1[:, :], xstat[:, :, 0])
                    dve.wait_ge(gexp_ok, 1)
                    link(V.tensor_scalar(gates[:, :], gates[:, :], 1.0, None, ALU.add))
                    link(V.reciprocal(gates[:, :], gates[:, :]))
                    V.tensor_scalar(gates[:, :], gates[:, :], -2.0, 1.0, ALU.mult, ALU.add).then_inc(gates_ok, 1)
                    dve.wait_ge(gates_ok, 1)
                elif name in ("mix0", "mix1"):
                    h = int(name[-1])
                    if h == 0:
                        dve.wait_ge(du_ok, b + 1)
                        dve.wait_ge(b_full, k + 1)
                    if k >= 3:
                        dve.wait_ge(red_ok, HALVES * (k - 3) + h + 1)
                    l0, ln, s0, sn = group(b, i)
                    V.tensor_tensor(states(hb[:, k % 3, h], b, i), states(b_ps[:, :, :].rearrange("p c m -> p (c m)"), b, i),
                                    du[:, p, h, l0:l0 + ln].unsqueeze(1).broadcast_to([P, sn, ln]),
                                    ALU.mult).then_inc(b_free, 1)
                elif name in ("scan0", "scan1"):
                    h = int(name[-1])
                    if k == 0:
                        dve.wait_ge(dA_zero, 1)
                    dve.wait_ge(dA_ok, HALVES * k + h + 1)
                    dve.wait_ge(b_free, HALVES * k + h + 1)
                    if b == BATCH - 1 and i >= 2:
                        s0, sn = group(b, i)[2:]
                        first_col = states(hb[:, k % 3, h], b, i)[:, :, 0]
                        dve.wait_ge(carry_ok, HALVES * (i - 2) + h + 1)
                        link(V.tensor_tensor(first_col, first_col, carry[:, h, s0:s0 + sn], ALU.add))
                    V.tensor_tensor_scan(hb[:, k % 3, h], dA[:, k % 2, h].rearrange("p n l -> p (n l)"),
                                         hb[:, k % 3, h], 0.0, ALU.mult, ALU.add).then_inc(scan_ok, 1)
                elif name == "yz":
                    dve.wait_ge(red_ok, HALVES * (NG * b + summed(b, i)))
                    dve.wait_ge(sz_ok, b + 1)
                    l = tokens(b, i)
                    V.tensor_tensor(yz[:, p, :, l], y_ps[:, :, l], ze[:, p, :, l], ALU.mult).then_inc(yz_ok, 1)
                elif name == "x1":
                    dve.wait_ge(work_full, full("yT", b, i))
                    t0, t1 = tiles(b, i)[0], tiles(b, i)[-1] + 1
                    xb = x[:, b, t0:t1].rearrange("p h l -> p (h l)")
                    V.scalar_tensor_tensor(out=xb, in0=bank("yT", b, i)[:, 0:(t1 - t0) * DI], scalar=gates[:, 0:1], in1=xb,
                                           op0=ALU.mult, op1=ALU.add).then_inc(free["dve"], 1)
                    dve.wait_ge(free["dve"], emptied("yT", b, i))
                    for h in range(t0, t1):
                        at = mark(V.bn_stats(fstat[:, h], x[:, b, h]))
                    dve.wait_ge(dve_k, at)
                    for h in range(t0, t1):
                        at = mark(V.bn_aggr(fmv[:, b, h], fstat[:, h]))
                    dve.wait_ge(dve_k, at)
                    V.tensor_scalar(fs[:, b, t0:t1], fmv[:, b, t0:t1, 1], EPS, None, ALU.add).then_inc(fmv_ok, 1)
                    for h in range(t0, t1):
                        at = mark(V.tensor_scalar(xn[:, h], x[:, b, h], fmv[:, b, h, 0:1], None, ALU.subtract))
                    dve.wait_ge(dve_k, at)
                    famx[b, i] = mark(V.tensor_reduce(fam[:, b, t0:t1], xn[:, t0:t1, :], AX.X, ALU.max, apply_absolute_value=True))
                elif name == "quant1":
                    t0, t1 = tiles(b, i)[0], tiles(b, i)[-1] + 1
                    ts = slice(t0, t1)
                    dve.wait_ge(dve_k, famx[b, i])
                    link(V.tensor_scalar(fam[:, b, ts], fam[:, b, ts], 1.0 / 127.0, None, ALU.mult))
                    dve.wait_ge(frs_ok, b + i + 1)
                    link(V.scalar_tensor_tensor(out=fam[:, b, ts], in0=fsd[:, b, ts], scalar=1e-5 / 127.0,
                                                in1=fam[:, b, ts], op0=ALU.mult, op1=ALU.max))
                    link(V.reciprocal(fs[:, b, ts], fam[:, b, ts]))
                    for h in range(t0, t1):
                        V.tensor_scalar(xn[:, h], xn[:, h], fs[:, b, h:h + 1], MAGIC, ALU.mult, ALU.add).then_inc(xqm_ok, 1)
                    V.tensor_tensor(finv[:, b, ts], fam[:, b, ts], frs[:, b, ts], ALU.mult).then_inc(finv_ok, 1)
                elif name == "gate":
                    h, c = i // 2, i % 2
                    dve.wait_ge(work_full, full("up", b, i, 1))
                    dve.wait_ge(free["act"], emptied("up", b, i, 0))
                    V.scalar_tensor_tensor(out=gg[:, p, h, c * UC:(c + 1) * UC], in0=bank("up", b, i, 1)[:, 0:UC],
                                           scalar=finv[:, b, h:h + 1], in1=ru[:, p, h, c * UC:(c + 1) * UC],
                                           op0=ALU.mult, op1=ALU.mult).then_inc(free["dve"], 1)
                elif name == "absmax":
                    dve.wait_ge(gw_ok[i], b + 1)
                    at = mark(V.tensor_reduce(gam[:, b, i:i + 1], gw[:, p, i], AX.X, ALU.max, apply_absolute_value=True))
                    if b == BATCH - 1 or i == HALVES - 1:
                        hs = slice(i, i + 1) if b == BATCH - 1 else slice(0, HALVES)
                        dve.wait_ge(ssq_ok[i], b + 1)
                        V.tensor_scalar(gv[:, b, hs], ssq[:, b, hs], 1.0 / HID, EPS, ALU.mult, ALU.add).then_inc(gv_ok, 1)
                        dve.wait_ge(dve_k, at)
                        gamx[b, hs.start] = mark(V.tensor_scalar(gam[:, b, hs], gam[:, b, hs], 1.0 / 127.0, None, ALU.mult))
                elif name == "scale2":
                    hs = slice(i, i + 1) if b == BATCH - 1 else slice(0, HALVES)
                    dve.wait_ge(grs_ok, b + 1 + i)
                    dve.wait_ge(dve_k, gamx[b, i])
                    link(V.scalar_tensor_tensor(out=gt[:, b, hs], in0=gsd[:, b, hs], scalar=1e-5 / 127.0,
                                                in1=gam[:, b, hs], op0=ALU.mult, op1=ALU.max))
                    link(V.reciprocal(gc[:, b, hs], gt[:, b, hs]))
                    if b == 0:
                        link(V.memset(ru[:, :, :, HID:HPAD], MAGIC))
                elif name == "outscale":
                    hs = slice(i, i + 1) if b == BATCH - 1 else slice(0, HALVES)
                    newton(grs[:, b, hs], gv[:, b, hs], gos[:, b, hs])
                    link(V.scalar_tensor_tensor(out=gos[:, b, hs], in0=gt[:, b, hs], scalar=gates[:, 1:2],
                                                in1=grs[:, b, hs], op0=ALU.mult, op1=ALU.mult))
                elif name == "quant2":
                    V.tensor_scalar(ru[:, p, i, 0:HID], gw[:, p, i], gc[:, b, i:i + 1], MAGIC, ALU.mult, ALU.add).then_inc(iq_ok, 1)
                elif name == "final":
                    t = HALVES * b + i
                    dve.wait_ge(work_full, full("down", b, i))
                    if t >= 2:
                        dve.wait_ge(stored[t % 2], 16 * (t // 2))
                    V.scalar_tensor_tensor(out=fin[:, t % 2], in0=bank("down", b, i)[:, 0:L], scalar=gos[:, b, i:i + 1],
                                           in1=x[:, b, i], op0=ALU.mult, op1=ALU.add).then_inc(free["dve"], 1)

        @block.tensor
        def _(pe):
            T = nc.tensor

            def claim(name, b, i, n=0):
                w = WORK_AT[(name, b, i, n)]
                if w >= NWORK:
                    who, count = WORK_BY[w - NWORK]
                    pe.wait_ge(free[who], count)
                return bank(name, b, i, n)

            pe.wait_ge(pool_k, 4)
            for name, b, i in ORDER["pe"]:
                p = b % 2
                k = b * NG + i
                if name == "warm":
                    if i == 1:
                        pe.wait_ge(conv_e, 1)
                    for j in range(WARM[i]):
                        T.transpose(y_ps[:, 0, 0:P], identf[:, :], identf[:, :])
                elif name == "winT":
                    pe.wait_ge(l_win, 16)
                    ps = claim("winT", 0, 0)
                    for h in range(HALVES):
                        last = T.transpose(ps[:, h * P:(h + 1) * P], win_in[:, h, :], identf[:, :])
                    last.then_inc(work_full, 1)
                elif name == "xpwT":
                    pe.wait_ge(l_xpw, 64)
                    ps = claim("xpwT", 0, 0)
                    for h in range(HALVES):
                        last = T.transpose(ps[:, h * P:(h + 1) * P], xpw_in[:, h * P:(h + 1) * P], identf[:, :])
                    last.then_inc(work_full, 1)
                elif name == "dtwT":
                    pe.wait_ge(l_dtw, 16)
                    ps = claim("dtwT", 0, 0)
                    for h in range(HALVES):
                        last = T.transpose(ps[0:RANK, h * P:(h + 1) * P], dtw_in[:, h, :], identf[:, :])
                    last.then_inc(work_full, 1)
                elif name == "ctxT":
                    pe.wait_ge(l_ctx0 if b == 0 else l_ctx, 16)
                    ps = claim(name, b, i)
                    for h in range(HALVES):
                        last = T.transpose(ps[:, h * P:(h + 1) * P], ctx_in[:, HALVES * b + h, :], identf[:, :])
                    last.then_inc(work_full, 1)
                elif name == "inproj":
                    pe.wait_ge(free["act"], emptied("ctxT", b, i))
                    if b == 0:
                        pe.wait_ge(free["act"], emptied("winT", 0, 0))
                    ps = claim(name, b, i)
                    for h in range(HALVES):
                        last = T.matmul(ps[:, h * L:(h + 1) * L], winT[:, h * P:(h + 1) * P], ctxT[:, p], start=True, stop=True)
                    last.then_inc(work_full, 1)
                elif name == "xdbl":
                    pe.wait_ge(u_ok, b + 1)
                    if b == 0:
                        pe.wait_ge(free["act"], emptied("xpwT", 0, 0))
                    ps = claim(name, b, i)
                    for h in range(HALVES):
                        last = T.matmul(ps[:, 0:L], xpwT[:, h], u[:, p, h], start=(h == 0), stop=(h == HALVES - 1))
                    last.then_inc(work_full, 1)
                elif name == "dtproj":
                    pe.wait_ge(dtlow_ok, b + 1)
                    if b == 0:
                        pe.wait_ge(free["dve"], emptied("dtwT", 0, 0))
                    ps = claim(name, b, i)
                    for h in range(HALVES):
                        last = T.matmul(ps[:, h * L:(h + 1) * L], dtwT[:, h * P:(h + 1) * P], dtlow[:, p], start=True, stop=True)
                    last.then_inc(work_full, 1)
                elif name == "bc_b":
                    pe.wait_ge(bcs_ok, b + 1)
                    if k == 0:
                        pe.wait_ge(sel_ok, 1)
                    if k:
                        pe.wait_ge(b_free, HALVES * k)
                    l0, ln, s0, sn = group(b, i)
                    for c in range(2):
                        for s in range(sn // 2):
                            last = T.matmul(b_ps[:, c, s * ln:(s + 1) * ln], sel[:, s0 + sn // 2 * c + s],
                                            bcs[:, p, l0:l0 + ln], start=True, stop=True)
                    last.then_inc(b_full, 1)
                elif name == "bc_c":
                    pe.wait_ge(bcs_ok, b + 1)
                    if k == 0:
                        pe.wait_ge(sel_ok, 1)
                    l0, ln, s0, sn = group(b, i)
                    for c in range(2):
                        if k:
                            pe.wait_ge(cs_ok, 2 * (k - 1) + c + 1)
                        for s in range(sn // 2):
                            last = T.matmul(c_ps[:, c, s * ln:(s + 1) * ln], sel[:, NS + s0 + sn // 2 * c + s],
                                            bcs[:, p, l0:l0 + ln], start=True, stop=True)
                        last.then_inc(c_full, 1)
                elif name == "skip":
                    if b == 0:
                        pe.wait_ge(diag_ok, HALVES)
                    if b + i:
                        pe.wait_ge(yz_ok, b + i)
                    pe.wait_ge(u_ok, b + 1)
                    l = tokens(b, i)
                    for h in range(HALVES):
                        T.matmul(y_ps[:, h, l], diag[:, h], u[:, p, h, l], start=(h == 0), stop=False,
                                 skip_group_check=True)
                elif name in ("sum0", "sum1"):
                    h = int(name[-1])
                    l0, ln, s0, sn = group(b, i)
                    if (b, i, h) == OUT_END:
                        pe.wait_ge(hc_end, 1)
                    else:
                        pe.wait_ge(hc_ok[h], k + 1)
                    for s in range(sn):
                        last = T.matmul(y_ps[:, h, l0:l0 + ln], identf[:, :], hb[:, k % 3, h, s * ln:(s + 1) * ln],
                                        start=False, stop=(s0 + s == NS - 1), skip_group_check=True)
                    last.then_inc(red_ok, 1)
                elif name == "yT":
                    pe.wait_ge(yz_ok, b + i + 1)
                    ps = claim(name, b, i)
                    for n, t in enumerate(tiles(b, i)):
                        for h in range(HALVES):
                            c = n * DI + h * P
                            last = T.transpose(ps[:, c:c + P], yz[:, p, h, t * P:(t + 1) * P], identf[:, :])
                    last.then_inc(work_full, 1)
                elif name == "xqT":
                    pe.wait_ge(xqm_ok, HALVES * b + tiles(b, i)[-1] + 1)
                    ps = claim(name, b, i)
                    for kh in range(HALVES):
                        for h in tiles(b, i):
                            c = (kh * HALVES + h) * P
                            last = T.transpose(ps[:, c:c + P], xn[:, h, kh * P:(kh + 1) * P], identf[:, :])
                    last.then_inc(work_full, 1)
                elif name == "up":
                    h, c = i // 2, i % 2
                    pe.wait_ge(free["act"], emptied("xqT", b, h if b == BATCH - 1 else 0))
                    if b == 0 and i == 0:
                        pe.wait_ge(wlo_ok, NWP)
                    for j in range(2):
                        ps = claim(name, b, i, j)
                        c0 = j * HID + c * UC
                        for kh in range(HALVES):
                            for s in range(3):
                                last = T.matmul(ps[:, 0:UC], xqT[:, kh, h, :], w13T[:, s, kh, c0:c0 + UC],
                                                start=(kh == 0 and s == 0), stop=(kh == 1 and s == 2))
                        last.then_inc(work_full, 1)
                elif name == "iqT":
                    pe.wait_ge(iq_ok, HALVES * b + i + 1)
                    for c in range(2):
                        ps = claim(name, b, i, c)
                        for f in range(3):
                            last = T.transpose(ps[:, f * P:(f + 1) * P], ru[:, p, i, (3 * c + f) * P:(3 * c + f + 1) * P],
                                               identf[:, :])
                        last.then_inc(work_full, 1)
                elif name == "down":
                    ps = claim(name, b, i)
                    for f in range(FB):
                        if f % 3 == 0:
                            pe.wait_ge(free["act"], emptied("iqT", b, i, f // 3))
                        for s in range(3):
                            last = T.matmul(ps[:, 0:DI], iqT[:, p, i, f, :], w2T[:, s, f * DI:(f + 1) * DI],
                                            start=(f == 0 and s == 0), stop=(f == FB - 1 and s == 2))
                    last.then_inc(work_full, 1)
                elif name == "w":
                    ps = claim(name, b, i)
                    if i < 6:
                        pe.wait_ge(l_w13, 16)
                        kh, t0 = i // 3, (i % 3) * 4
                        for t in range(t0, min(t0 + 4, 11)):
                            last = T.transpose(ps[:, (t - t0) * P:(t - t0 + 1) * P], w13_in[:, t, kh * P:(kh + 1) * P],
                                               identf[:, :])
                    else:
                        pe.wait_ge(l_w2, 16)
                        pe.wait_ge(pool_k, 5)
                        for j in range(4):
                            f, h = 2 * (i - 6) + j // 2, j % 2
                            last = T.transpose(ps[:, j * P:(j + 1) * P], w2_in[:, h, f * P:(f + 1) * P], identf[:, :])
                    last.then_inc(work_full, 1)


def kernel(**inputs):
    import numpy as np
    import concourse.bacc as bacc
    from concourse.bass_utils import run_bass_kernel_spmd

    nc = bacc.Bacc("TRN2", target_bir_lowering=False, num_devices=1)
    arrays, args = {}, {}
    for name, v in inputs.items():
        v = np.ascontiguousarray(v)
        arrays["in_" + name] = v
        args[name] = nc.dram_tensor("in_" + name, v.shape, mybir.dt.from_np(v.dtype), kind="ExternalInput").ap()
    out = nc.dram_tensor("out", (BATCH, L, DI), fp32, kind="ExternalOutput").ap()
    build(nc, args, out)
    r = run_bass_kernel_spmd(nc, [arrays], core_ids=[0])
    return r.results[0]["out"]
```
